# Optimizing a Trainium2 kernel written in Bass

```python
import numpy as np
import jax
import jax.numpy as jnp

def _softmax(x, axis=-1):
    return jax.nn.softmax(x, axis=axis)

def _gelu(x):
    return jax.nn.gelu(x, approximate=True)

def _silu(x):
    return jax.nn.silu(x)

def _sigmoid(x):
    return jax.nn.sigmoid(x)

def _layernorm(x, axis=-1, eps=1e-05):
    m = jnp.mean(x, axis=axis, keepdims=True)
    v = jnp.var(x, axis=axis, keepdims=True)
    return (x - m) / jnp.sqrt(v + eps)

def _scatter_add(tgt, idx, src, axis=0):
    return tgt.at[idx].add(src)

def _segment_sum(src, seg, n):
    return jax.ops.segment_sum(src, seg, n)
kernel_name = 'mk_conv_seq_d2_conv_nhwc128_r2_6e53fd'

def setup_inputs(seed: int=0):
    np.random.seed(seed)
    _w = jnp.asarray

    def _rec_inputs():
        import jax
        import jax.numpy as jnp
        _gk = jax.random.key(seed)
        x = -0.000125 + 0.9999 * jax.random.normal(jax.random.fold_in(_gk, 1), (1, 256, 256, 64), jnp.float32)
        return x
    x = _rec_inputs()

    def _L0_conv_setup():
        import jax, jax.numpy as jnp
        import numpy as np
        C_Z = 64
        C_HID = 64

        def _layer_norm(x, w, b, eps=1e-05):
            mu = jnp.mean(x, axis=-1, keepdims=True)
            var = jnp.mean(jnp.square(x - mu), axis=-1, keepdims=True)
            return (x - mu) * jax.lax.rsqrt(var + eps) * w + b
        key = jax.random.key(seed)
        ks = jax.random.split(key, 8)
        B, N = (1, 256)
        z = jax.random.normal(ks[0], (B, N, N, C_Z), dtype=jnp.float32)
        mask = jnp.ones((B, N, N), dtype=jnp.float32)
        s = 0.02
        params = {'ln_w': jnp.ones((C_Z,), jnp.float32), 'ln_b': jnp.zeros((C_Z,), jnp.float32), 'W_ap': jax.random.normal(ks[1], (C_Z, C_HID), jnp.float32) * s, 'b_ap': jnp.zeros((C_HID,), jnp.float32), 'W_ag': jax.random.normal(ks[2], (C_Z, C_HID), jnp.float32) * s, 'b_ag': jnp.zeros((C_HID,), jnp.float32), 'W_bp': jax.random.normal(ks[3], (C_Z, C_HID), jnp.float32) * s, 'b_bp': jnp.zeros((C_HID,), jnp.float32), 'W_bg': jax.random.normal(ks[4], (C_Z, C_HID), jnp.float32) * s, 'b_bg': jnp.zeros((C_HID,), jnp.float32), 'W_z': jax.random.normal(ks[5], (C_HID, C_Z), jnp.float32) * s, 'b_z': jnp.zeros((C_Z,), jnp.float32)}
        return {'z': z, 'mask': mask, **params}
    _L0_conv_all = _L0_conv_setup()
    _L0_conv_in = {k: v for k, v in _L0_conv_all.items() if k in ('mask', 'ln_w', 'ln_b', 'W_ap', 'b_ap', 'W_ag', 'b_ag', 'W_bp', 'b_bp', 'W_bg', 'b_bg', 'W_z', 'b_z')}
    del _L0_conv_all

    def _L1_conv_setup():
        import jax, jax.numpy as jnp
        import numpy as np
        EPS = 1e-05

        def _layernorm(x, w, b):
            m = jnp.mean(x, axis=-1, keepdims=True)
            v = jnp.mean(jnp.square(x - m), axis=-1, keepdims=True)
            return (x - m) * jax.lax.rsqrt(v + EPS) * w + b
        key = jax.random.key(seed)
        ks = jax.random.split(key, 8)
        N, S, Z, E = (1, 256, 64, 64)
        scale = 0.02
        return {'pair_repr': jax.random.normal(ks[0], (N, S, S, Z), dtype=jnp.float32), 'ln1_w': jnp.ones((Z,), jnp.float32), 'ln1_b': jnp.zeros((Z,), jnp.float32), 'left1': jax.random.normal(ks[1], (Z, E), jnp.float32) * scale, 'left2': jax.random.normal(ks[2], (Z, E), jnp.float32) * scale, 'right1': jax.random.normal(ks[3], (Z, E), jnp.float32) * scale, 'right2': jax.random.normal(ks[4], (Z, E), jnp.float32) * scale, 'ln2_w': jnp.ones((E,), jnp.float32), 'ln2_b': jnp.zeros((E,), jnp.float32), 'out_w': jax.random.normal(ks[5], (E, Z), jnp.float32) * scale, 'gate': jax.random.normal(ks[6], (Z, Z), jnp.float32) * scale}
    _L1_conv_all = _L1_conv_setup()
    _L1_conv_in = {k: v for k, v in _L1_conv_all.items() if k in ('ln1_w', 'ln1_b', 'left1', 'left2', 'right1', 'right2', 'ln2_w', 'ln2_b', 'out_w', 'gate')}
    del _L1_conv_all
    return {'x': x, 'L0_conv_mask': _L0_conv_in['mask'], 'L0_conv_ln_w': _L0_conv_in['ln_w'], 'L0_conv_ln_b': _L0_conv_in['ln_b'], 'L0_conv_W_ap': _L0_conv_in['W_ap'], 'L0_conv_b_ap': _L0_conv_in['b_ap'], 'L0_conv_W_ag': _L0_conv_in['W_ag'], 'L0_conv_b_ag': _L0_conv_in['b_ag'], 'L0_conv_W_bp': _L0_conv_in['W_bp'], 'L0_conv_b_bp': _L0_conv_in['b_bp'], 'L0_conv_W_bg': _L0_conv_in['W_bg'], 'L0_conv_b_bg': _L0_conv_in['b_bg'], 'L0_conv_W_z': _L0_conv_in['W_z'], 'L0_conv_b_z': _L0_conv_in['b_z'], 'L1_conv_ln1_w': _L1_conv_in['ln1_w'], 'L1_conv_ln1_b': _L1_conv_in['ln1_b'], 'L1_conv_left1': _L1_conv_in['left1'], 'L1_conv_left2': _L1_conv_in['left2'], 'L1_conv_right1': _L1_conv_in['right1'], 'L1_conv_right2': _L1_conv_in['right2'], 'L1_conv_ln2_w': _L1_conv_in['ln2_w'], 'L1_conv_ln2_b': _L1_conv_in['ln2_b'], 'L1_conv_out_w': _L1_conv_in['out_w'], 'L1_conv_gate': _L1_conv_in['gate']}

def reference(x, L0_conv_mask, L0_conv_ln_w, L0_conv_ln_b, L0_conv_W_ap, L0_conv_b_ap, L0_conv_W_ag, L0_conv_b_ag, L0_conv_W_bp, L0_conv_b_bp, L0_conv_W_bg, L0_conv_b_bg, L0_conv_W_z, L0_conv_b_z, L1_conv_ln1_w, L1_conv_ln1_b, L1_conv_left1, L1_conv_left2, L1_conv_right1, L1_conv_right2, L1_conv_ln2_w, L1_conv_ln2_b, L1_conv_out_w, L1_conv_gate):
    import jax
    import jax.numpy as jnp

    def _L0_conv_ref(z, mask, ln_w, ln_b, W_ap, b_ap, W_ag, b_ag, W_bp, b_bp, W_bg, b_bg, W_z, b_z):
        import jax, jax.numpy as jnp
        import numpy as np
        C_Z = 64
        C_HID = 64

        def _layer_norm(x, w, b, eps=1e-05):
            mu = jnp.mean(x, axis=-1, keepdims=True)
            var = jnp.mean(jnp.square(x - mu), axis=-1, keepdims=True)
            return (x - mu) * jax.lax.rsqrt(var + eps) * w + b
        z_norm = _layer_norm(z, ln_w, ln_b)
        m = mask[..., None]
        a = (z_norm @ W_ap + b_ap) * jax.nn.sigmoid(z_norm @ W_ag + b_ag) * m
        b = (z_norm @ W_bp + b_bp) * jax.nn.sigmoid(z_norm @ W_bg + b_bg) * m
        out = jnp.einsum('bikc,bkjc->bijc', a, b)
        return z + (out @ W_z + b_z)

    def _L1_conv_ref(pair_repr, ln1_w, ln1_b, left1, left2, right1, right2, ln2_w, ln2_b, out_w, gate):
        import jax, jax.numpy as jnp
        import numpy as np
        EPS = 1e-05

        def _layernorm(x, w, b):
            m = jnp.mean(x, axis=-1, keepdims=True)
            v = jnp.mean(jnp.square(x - m), axis=-1, keepdims=True)
            return (x - m) * jax.lax.rsqrt(v + EPS) * w + b
        residual = pair_repr
        x = _layernorm(pair_repr, ln1_w, ln1_b)
        left = jax.nn.sigmoid(x @ left1) * (x @ left2)
        right = jax.nn.sigmoid(x @ right1) * (x @ right2)
        p = jnp.einsum('nsre,nkre->nske', left, right)
        p = _layernorm(p, ln2_w, ln2_b)
        g = jax.nn.sigmoid(jnp.einsum('nsrz,zy->nsry', x, gate))
        q = jnp.einsum('nrse,ez->nsrz', p, out_w) * g
        return residual + q

    def _gn(v, G=32, eps=1e-05):
        B_, H_, W_, C_ = v.shape
        g = v.reshape(B_, H_, W_, G, C_ // G)
        m = jnp.mean(g, axis=(1, 2, 4), keepdims=True)
        s = jnp.var(g, axis=(1, 2, 4), keepdims=True)
        return ((g - m) / jnp.sqrt(s + eps)).reshape(v.shape)

    def _ln_c(v, eps=1e-06):
        m = jnp.mean(v, axis=-1, keepdims=True)
        s = jnp.var(v, axis=-1, keepdims=True)
        return (v - m) / jnp.sqrt(s + eps)

    def _ln_t(v, eps=1e-05):
        m = jnp.mean(v, axis=-1, keepdims=True)
        s = jnp.var(v, axis=-1, keepdims=True)
        return (v - m) / jnp.sqrt(s + eps)

    def _to_tokens(v):
        B_, H_, W_, C_ = v.shape
        return v.reshape(B_, H_ * W_, C_)

    def _from_tokens(t, like):
        return t.reshape(like.shape)
    x = _L0_conv_ref(x, L0_conv_mask, L0_conv_ln_w, L0_conv_ln_b, L0_conv_W_ap, L0_conv_b_ap, L0_conv_W_ag, L0_conv_b_ag, L0_conv_W_bp, L0_conv_b_bp, L0_conv_W_bg, L0_conv_b_bg, L0_conv_W_z, L0_conv_b_z)
    x = _L1_conv_ref(x, L1_conv_ln1_w, L1_conv_ln1_b, L1_conv_left1, L1_conv_left2, L1_conv_right1, L1_conv_right2, L1_conv_ln2_w, L1_conv_ln2_b, L1_conv_out_w, L1_conv_gate)
    return x

_drawn_inputs = setup_inputs


def setup_inputs(seed=0):
    import zlib

    import numpy as np

    out = dict(_drawn_inputs(seed))
    spreads = {'L0_conv_ln_w': (1.0, 0.6),
     'L0_conv_ln_b': (0.0, 0.313),
     'L0_conv_b_ap': (0.0, 0.1),
     'L0_conv_b_ag': (0.0, 2.0),
     'L0_conv_b_bp': (0.0, 0.1),
     'L0_conv_b_bg': (0.0, 0.8),
     'L0_conv_b_z': (0.0, 0.1),
     'L1_conv_ln1_w': (1.0, 0.6),
     'L1_conv_ln1_b': (0.0, 0.291),
     'L1_conv_ln2_w': (1.0, 0.6),
     'L1_conv_ln2_b': (0.0, 0.8)}
    factors = {'L0_conv_W_ag': 8.0,
     'L0_conv_W_bg': 8.0,
     'L1_conv_left1': 8.0,
     'L1_conv_right1': 8.0,
     'L1_conv_gate': 8.0}
    for name, (base, spread) in spreads.items():
        noise = np.random.default_rng([zlib.crc32(name.encode()), seed]).standard_normal(out[name].shape)
        drawn = base * np.exp(spread * noise) if base else spread * noise
        out[name] = jnp.asarray(drawn.astype(out[name].dtype))
    for name, factor in factors.items():
        out[name] = (out[name] * factor).astype(out[name].dtype)
    return out
```

```python
from contextlib import ExitStack

import concourse.bass as bass
from concourse import mybir

F32 = mybir.dt.float32
BF16 = mybir.dt.bfloat16
ALU = mybir.AluOpType
ACT = mybir.ActivationFunctionType

P = 128
C = 64
N = 256
HALVES = N // P
EPS = 1e-5
COLS = 8
STEPS = P // COLS
GRP = 16
GROUPS = P // GRP
CHUNKS = HALVES * GROUPS
UNROLL = 4
LAG = 4
CG = 8
START = 4


def after(step):
    return START + 1 + step


SEGMENTS = [
    dict(norm=("z", 0, 0), gen=None, contract=False),
    dict(norm=("z", 1, 0), gen=None, contract=False),
    dict(norm=("z", 0, 1), gen=(0, "rhs", "col", 0), contract=False),
    dict(norm=("z", 1, 1), gen=(0, "lhs", "row", 0), contract=True),
    dict(norm=("x", 0, 0), gen=(0, "lhs", "row", 1), contract=True),
    dict(norm=("x", 1, 0), gen=(0, "rhs", "col", 1), contract=True),
    dict(norm=("x", 1, 1), gen=(0, "lhs", "row", 0), contract=True),
    dict(norm=("x", 0, 1), gen=(1, "lhs", "row", 1), contract=False),
    dict(norm=None, gen=(1, "rhs", "row", 1), contract=True),
    dict(norm=("p", 1, 1), gen=(1, "rhs", "row", 0), contract=True),
    dict(norm=("p", 1, 0), gen=(1, "lhs", "row", 0), contract=True),
    dict(norm=("p", 0, 0), gen=(1, "rhs", "row", 1), contract=True),
    dict(norm=("p", 0, 1), gen=None, contract=False),
]
X_BASE = 4 * STEPS
P_BASE = 8 * STEPS
GROUPS_C = C // CG


def number_segments():
    m = k = e = rows = cols = 0
    for seg in SEGMENTS:
        seg.update(m0=m, k0=k, e0=e, rows0=rows, cols0=cols)
        m += STEPS if seg["norm"] else 0
        k += CHUNKS if seg["gen"] else 0
        rows += CHUNKS if seg["gen"] and seg["gen"][2] == "row" else 0
        cols += CHUNKS if seg["gen"] and seg["gen"][2] == "col" else 0
        e += GROUPS_C if seg["contract"] else 0


number_segments()


ROUNDS = STEPS // UNROLL


def walk(eng, seg, body, before_tail=None):
    def looking_back(r, j):
        def at(lag):
            back = j < lag
            r1, j1 = (r - 1, j - lag + UNROLL) if back else (r, j - lag)
            if isinstance(r, int) and not 0 <= r1 < ROUNDS:
                return None
            return r1, j1
        return at

    for j in range(UNROLL):
        body(looking_back(0, j))
    with eng.Fori(1, ROUNDS, 1) as r:
        for j in range(UNROLL):
            body(looking_back(r, j))
    if before_tail:
        before_tail()
    if seg["norm"]:
        for j in range(LAG):
            body(looking_back(ROUNDS, j), tail=True)


def number(r, j):
    return UNROLL * r + j


def triangle_layers(nc, x, mask, ln_w, ln_b, W_ap, b_ap, W_ag, b_ag, W_bp, b_bp, W_bg, b_bg,
                    W_z, b_z, ln1_w, ln1_b, left1, left2, right1, right2, ln2_w, ln2_b, out_w,
                    gate, out):
    x3, out3 = x[0], out[0]
    xt_dram = [nc.dram_tensor(f"xt{n}", [HALVES, P, GROUPS, N, GRP], BF16).ap() for n in range(2)]
    x1_dram = nc.dram_tensor("x1", [N, N, C], F32).ap()

    with ExitStack() as ctx:
        def sb(name, shape, dt=F32):
            return ctx.enter_context(nc.sbuf_tensor(name, shape, dt))

        def sem(name):
            return ctx.enter_context(nc.semaphore(name))

        operand = {"lhs": sb("lhs", [P, HALVES, C, P]), "rhs": sb("rhs", [P, HALVES, C, P])}
        quad = sb("quad", [P, P, C])
        chunk = sb("chunk", [P, 2, P * GRP], BF16)
        sig = sb("sig", [P, 2, COLS, C])
        masks = sb("masks", [P, 2, HALVES, N])
        mask_kj, mask_ki = masks[:, 0], masks[:, 1]
        xin = sb("xin", [P, 4, COLS, C])
        xc = sb("xc", [P, 2, COLS, C])
        split = sb("split", [P, 2, COLS, 2, C], BF16)
        gt = split[:, :, :, :, :].bitcast(F32).rearrange("p b t a c -> p b t (a c)")
        xt = sb("xt", [P, 2, GROUPS, GRP, GRP], BF16)
        gchunk = xt[:, 0].rearrange("p g j r -> p (g j r)")
        gspread = [xt[:, 1].rearrange("p g j r -> p (g j r)"),
                   masks[:, :, :, :].rearrange("p a h n -> p (a h n)").bitcast(BF16)]
        opair = sb("opair", [P, COLS // 2, P])
        stats = sb("stats", [P, 2, COLS, 3])
        rstd = sb("rstd", [P, 2, COLS])
        var = sb("var", [P, 2, COLS])
        ident = sb("ident", [P, P])
        ident_b = sb("ident_b", [P, P], BF16)
        ones_b = sb("ones_b", [P, P], BF16)
        w_lhs = [sb(f"w_lhs{n}", [P, 2, 2 * C], BF16) for n in range(2)]
        w_rhs = [sb(f"w_rhs{n}", [P, 2, 2 * C], BF16) for n in range(2)]
        w_gate = sb("w_gate", [P, 2, C], BF16)
        w_out = [sb(f"w_out{n}", [P, P]) for n in range(2)]
        bz_rows = sb("bz_rows", [P, C], BF16)
        ln2 = sb("ln2", [P, 2])
        eps = sb("eps", [P, 1])
        minus_half = sb("minus_half", [P, COLS])

        banks = [ctx.enter_context(nc.psum_tensor(f"bank{n}", [P, 2, 512], F32)) for n in range(2)]
        ps_t = ctx.enter_context(nc.psum_tensor("ps_t", [P, COLS // 2, P], F32))
        ps_w = ctx.enter_context(nc.psum_tensor("ps_w", [P, COLS, C], F32))
        ps_x = ctx.enter_context(nc.psum_tensor("ps_x", [P, 2, COLS, P], BF16))
        ps_g = ps_x[:, 0].bitcast(F32)

        loaded = sem("loaded")
        zeroed = sem("zeroed")
        idents = sem("idents")
        prep_v, prep_pe = sem("prep_v"), sem("prep_pe")
        ready = sem("ready")
        x_landed = [sem(f"x_landed{n}") for n in range(4)]
        x_stored = [sem(f"x_stored{n}") for n in range(4)]
        chunk_landed = [sem(f"chunk_landed{n}") for n in range(2)]
        cols_landed, gchunk_landed = sem("cols_landed"), sem("gchunk_landed")
        cols_spread, gate_spread = sem("cols_spread"), sem("gate_spread")
        xt_stored = [sem(f"xt_stored{n}") for n in range(2)]
        stats_done, centred, std_done = sem("stats_done"), sem("centred"), sem("std_done")
        var_done, rstd_done = sem("var_done"), sem("rstd_done")
        normed, high_done, low_done = sem("normed"), sem("high_done"), sem("low_done")
        x_turned, xt_done = sem("x_turned"), sem("xt_done")
        projected, gated, masked, made = sem("projected"), sem("gated"), sem("masked"), sem("made")
        contracted, quad_done = sem("contracted"), sem("quad_done")
        paired, turned, turned_out = sem("paired"), sem("turned"), sem("turned_out")
        mixed, added = sem("mixed"), sem("added")
        gate_mm, gate_sig, scaled, summed = (sem("gate_mm"), sem("gate_sig"), sem("scaled"),
                                             sem("summed"))

        scratch = quad[:, :, :].rearrange("p j c -> p (j c)")
        at = [0]

        def temp(rows, width):
            at[0] += width
            return scratch[0:rows, at[0] - width:at[0]]

        sets = [
            (w_lhs[0], W_ag, W_ap, b_ag, b_ap, 0), (w_rhs[0], W_bg, W_bp, b_bg, b_bp, 0),
            (w_lhs[1], right1, right2, None, None, 1), (w_rhs[1], left1, left2, None, None, 1),
            (w_gate, gate, None, None, None, 1),
        ]
        raw = [temp(C, C if s[2] is None else 2 * C) for s in sets]
        scaled_w = [temp(C, C if s[2] is None else 2 * C) for s in sets]
        bias_row = [temp(1, 2 * C) if s[3] is not None else None for s in sets]
        norm_w = [temp(C, 1) for _ in range(2)]
        norm_b = [temp(C, 1) for _ in range(2)]
        fold = temp(C, P)
        put_bias = [temp(C, P) for _ in range(2)]
        bz = temp(P, C)
        bz_rest = [temp(P, C) for _ in range(2)]
        bz_part = [temp(P, C // 2).bitcast(BF16) for _ in range(3)]
        prep_ps = [banks[0][:, 0, 0:2 * C], banks[0][:, 1, 0:2 * C], banks[1][:, 0, 0:2 * C],
                   banks[1][:, 1, 0:2 * C], ps_w[:, 0:2, :].rearrange("p a c -> p (a c)")]

        def column(v):
            return v.rearrange("(c a) -> c a", a=1)

        def row(v):
            return v.rearrange("(a c) -> a c", a=1)

        loads = []
        for n, (dst, wg, wv, bg, bv, layer) in enumerate(sets):
            loads.append((raw[n][:, 0:C], wg))
            if wv is not None:
                loads.append((raw[n][:, C:2 * C], wv))
            if bg is not None:
                loads += [(bias_row[n][:, 0:C], row(bg)), (bias_row[n][:, C:2 * C], row(bv))]
        for n, (w, b) in enumerate([(ln_w, ln_b), (ln1_w, ln1_b)]):
            loads += [(norm_w[n], column(w)), (norm_b[n], column(b))]
        for n, v in enumerate((ln2_w, ln2_b)):
            loads += [(ln2[h * C:(h + 1) * C, n:n + 1], column(v)) for h in range(2)]
        loads.append((bz, row(b_z).broadcast_to([P, C])))
        loads.append((mask_kj[:, :, :], mask[0].rearrange("(h p) j -> p h j", p=P)))
        loads_diag = [(w_out[n][h * C:(h + 1) * C, h * C:(h + 1) * C], w)
                      for n, w in enumerate((W_z, out_w)) for h in range(2)]
        LOADED = 16 * (len(loads) + len(loads_diag))

        block = ctx.enter_context(nc.Block())

        @block.sync
        def _(sp):
            for s in x_stored:
                sp.sem_inc(s, 16)
            for dst, src in loads:
                sp.dma_start(dst, src).then_inc(loaded, 16)
            sp.wait_ge(zeroed, 1)
            for dst, src in loads_diag:
                sp.dma_start(dst, src).then_inc(loaded, 16)

            def load_x(seg, r, j):
                kind, rh, ch = seg["norm"]
                m = seg["m0"] + number(r, j)
                if kind != "p":
                    sp.wait_ge(centred, after(m - 4))
                if kind != "z":
                    sp.wait_ge(x_stored[j], 16 * (r + (seg["m0"] - X_BASE) // 4 + 1))
                src = (x1_dram if kind == "p" else x3)
                sp.dma_start(xin[:, j], src[rh * P:(rh + 1) * P, bass.ds(ch * P + COLS * number(r, j), COLS), :]
                             ).then_inc(x_landed[j], 16)

            def load_chunk(seg, r, j):
                layer, _, kind, half = seg["gen"]
                group, other = 2 * r + j // 2, j % 2
                buf = chunk[:, j % 2 if kind == "row" else 0]
                if kind == "col" and not (isinstance(r, int) and (r, j) == (0, 0)):
                    sp.wait_ge(cols_spread, after(seg["cols0"] + number(r, j) - 1))
                else:
                    sp.wait_ge(projected, after(2 * (seg["k0"] + number(r, j) - 2) + 1))
                if kind == "row":
                    src = xt_dram[layer][half, :, bass.ds(group, 1), other * P:(other + 1) * P, :]
                    dst = buf.rearrange("p (g j r) -> p g j r", g=1, r=GRP)
                else:
                    src = xt_dram[layer][other, :, :, bass.ds(half * P + GRP * group, GRP), :]
                    dst = buf.rearrange("p (g j r) -> p g j r", g=GROUPS, r=GRP)
                sp.dma_start(dst, src).then_inc(chunk_landed[j % 2] if kind == "row" else cols_landed,
                                                16)

            def load_gate(seg, r, j):
                _, rh, ch = seg["norm"]
                sp.wait_ge(gate_spread, after((seg["m0"] - P_BASE) // 2 + 2 * r + j // 2 - 1))
                sp.dma_start(gchunk.rearrange("p (g j r) -> p g j r", g=GROUPS, r=GRP),
                             xt_dram[1][rh, :, :, bass.ds(ch * P + COLS * number(r, j), GRP), :]
                             ).then_inc(gchunk_landed, 16)

            def store_x(seg, r, j):
                kind, rh, ch = seg["norm"]
                m = seg["m0"] + number(r, j)
                if kind == "x":
                    sp.wait_ge(added, after(m - X_BASE))
                    dst = x1_dram
                else:
                    sp.wait_ge(summed, after(m - P_BASE))
                    dst = out3
                sp.dma_start(dst[rh * P:(rh + 1) * P, bass.ds(ch * P + COLS * number(r, j), COLS), :],
                             xin[:, j]).then_inc(x_stored[j], 16)

            def store_xt(seg, r, j):
                kind, rh, ch = seg["norm"]
                sp.wait_ge(xt_done, after(seg["m0"] + number(r, j)))
                sp.dma_start(xt_dram[kind == "x"][rh, :, :, bass.ds(ch * P + COLS * UNROLL * r + COLS * (j - 1), GRP), :],
                             xt[:, j // 2]).then_inc(xt_stored[j // 2], 16)

            def wait_stored(seg):
                pairs = min(seg["m0"], P_BASE) // 4
                if pairs:
                    for n in range(2):
                        sp.wait_ge(xt_stored[n], 16 * pairs)
                if seg["m0"] > X_BASE:
                    for n in range(4):
                        sp.wait_ge(x_stored[n], 16 + 16 * (seg["m0"] - X_BASE) // 4)

            for n, seg in enumerate(SEGMENTS):
                wait_stored(seg)
                if n and SEGMENTS[n - 1]["gen"] and SEGMENTS[n - 1]["gen"][2] == "col":
                    sp.wait_ge(projected, after(2 * seg["k0"] - 1))

                def body(at, tail=False, seg=seg):
                    if seg["gen"] and at(0):
                        load_chunk(seg, *at(0))
                    if not seg["norm"]:
                        return
                    kind = seg["norm"][0]
                    if kind == "p" and at(0) and at(0)[1] % 2 == 0:
                        load_gate(seg, *at(0))
                    if kind == "p" and at(4):
                        store_x(seg, *at(4))
                    if at(0):
                        load_x(seg, *at(0))
                    if kind == "x" and at(2):
                        store_x(seg, *at(2))
                    if kind != "p" and at(4) and at(4)[1] % 2 == 1:
                        store_xt(seg, *at(4))

                walk(sp, seg, body)
            for n in range(4):
                sp.wait_ge(x_stored[n], 16 + 16 * (3 * 4 * STEPS - X_BASE) // 4)

        @block.gpsimd
        def _(pool):
            g = nc.gpsimd
            for s in (centred, masked, summed, var_done):
                pool.sem_inc(s, START)
            g.memset(ident[:, :], 0.0).then_inc(idents, 1)
            for n in range(2):
                last = g.memset(w_out[n][:, :], 0.0)
            last.then_inc(zeroed, 1)
            g.memset(minus_half[:, :], -0.5)
            g.memset(eps[:, :], EPS)
            g.memset(ones_b[:, :], 1.0)
            pool.wait_ge(idents, 1)
            g.affine_select(out=ident[:, :], in_=ident[:, :], compare_op=ALU.not_equal, fill=1.0,
                            base=0, pattern=[[-1, P]], channel_multiplier=1).then_inc(idents, 1)
            pool.wait_ge(ready, 1)

            def mask_gate(seg, r, j):
                layer, op, kind, half = seg["gen"]
                group, other = 2 * r + j // 2, j % 2
                table = mask_ki if kind == "row" else mask_kj
                for s in range(2):
                    pool.wait_ge(gated, after(2 * (seg["k0"] + number(r, j)) + s))
                    col = half * P + GRP * group + COLS * s
                    m8 = table[:, other, bass.ds(col, COLS)].unsqueeze(2)
                    g.tensor_tensor(sig[:, s], sig[:, s], m8.broadcast_to([P, COLS, C]),
                                    ALU.mult).then_inc(masked, 1)

            def centre(seg, r, j):
                kind = seg["norm"][0]
                m, h = seg["m0"] + number(r, j), j % 2
                pool.wait_ge(stats_done, after(m))
                if kind == "p":
                    pool.wait_ge(turned, after(m - X_BASE - 2))
                else:
                    pool.wait_ge(low_done, after(m - 2))
                use_pow = not sqrt_on_act(seg)
                lo = 0 if kind == "p" else 1
                if kind == "p":
                    src = quad[:, bass.ds(COLS * number(r, j), COLS), :]
                else:
                    src = xin[:, j]
                last = g.tensor_tensor(xc[:, h, :, lo:], src[:, :, lo:],
                                       stats[:, h, :, 1:2].broadcast_to([P, COLS, C - lo]),
                                       ALU.subtract)
                if use_pow:
                    g.tensor_scalar(var[:, h], stats[:, h, :, 2], 1.0 / C, EPS, ALU.mult,
                                    ALU.add).then_inc(var_done, 1)
                    pool.wait_ge(var_done, after(m - POW_BASE))
                    last = g.tensor_tensor(rstd[:, h], var[:, h], minus_half[:, :], ALU.pow)
                last.then_inc(centred, 1)

            def add_residual(seg, r, j):
                m, h = seg["m0"] + number(r, j), j % 2
                pool.wait_ge(scaled, after(m - P_BASE))
                pool.wait_ge(x_landed[j], landed(seg, r))
                g.tensor_tensor(xin[:, j], xin[:, j], gt[:, h], ALU.add).then_inc(summed, 1)

            for seg in SEGMENTS:
                def gen_part(r, j, seg=seg):
                    if seg["gen"] and seg["gen"][0] == 0:
                        mask_gate(seg, r, j)

                def body(at, tail=False, seg=seg):
                    if at(1) and not tail:
                        gen_part(*at(1))
                    if not seg["norm"]:
                        return
                    if at(1):
                        centre(seg, *at(1))
                    if seg["norm"][0] == "p" and at(4):
                        add_residual(seg, *at(4))

                walk(pool, seg, body, before_tail=lambda: gen_part(ROUNDS - 1, UNROLL - 1))

        @block.scalar
        def _(act):
            a = nc.scalar
            for s in (std_done, high_done, gated, quad_done, paired, turned_out, gate_sig):
                act.sem_inc(s, START)
            act.wait_ge(ready, 1)

            def gates(seg, r, j):
                for s in range(2):
                    n = 2 * (seg["k0"] + number(r, j)) + s
                    act.wait_ge(projected, after(n))
                    act.wait_ge(made, after(n - 2))
                    v = banks[s][:, :, :].rearrange("p b (t c) -> p (b t) c", c=2 * C)
                    a.activation(sig[:, s], v[:, :, 0:C], ACT.Sigmoid).then_inc(gated, 1)

            def std(seg, r, j):
                m, h = seg["m0"] + number(r, j), j % 2
                act.wait_ge(stats_done, after(m))
                act.wait_ge(normed, after(m - 2))
                a.activation(var[:, h], stats[:, h, :, 2], ACT.Sqrt, scale=1.0 / C,
                             bias=eps[:, :]).then_inc(std_done, 1)

            def high(seg, r, j):
                m, h = seg["m0"] + number(r, j), j % 2
                act.wait_ge(normed, after(m))
                act.wait_ge(x_turned, after(m - 2))
                a.activation(split[:, h, :, 0, 1:], xc[:, h, :, 1:], ACT.Copy
                             ).then_inc(high_done, 1)

            def pair_up(seg, r, j):
                o = seg["m0"] - X_BASE + number(r, j)
                act.wait_ge(mixed, after(o - 1))
                a.activation(opair[:, :, :].rearrange("p a (b c) -> p (a b) c", c=C),
                             quad[:, bass.ds(COLS * number(r, j), COLS), :], ACT.Copy).then_inc(paired, 1)

            def turn_out(seg, r, j):
                o = seg["m0"] - X_BASE + number(r, j)
                act.wait_ge(turned, after(o))
                if seg["norm"][0] == "x":
                    a.activation(opair[:, :, :], ps_t[:, :, :], ACT.Copy).then_inc(turned_out, 1)
                else:
                    act.wait_ge(mixed, after(o - 1))
                    a.activation(opair[:, :, :], ps_t[:, :, :], ACT.Identity, scale=ln2[:, 0:1],
                                 bias=ln2[:, 1:2]).then_inc(turned_out, 1)

            def gate_out(seg, r, j):
                n, h = seg["m0"] - P_BASE + number(r, j), j % 2
                act.wait_ge(gate_mm, after(n))
                act.wait_ge(summed, after(n - 2))
                a.activation(gt[:, h], ps_g.rearrange("p t c -> p (t c)").rearrange("p (t c) -> p t c", c=C),
                             ACT.Sigmoid).then_inc(gate_sig, 1)

            for seg in SEGMENTS:
                kind = seg["norm"] and seg["norm"][0]
                if kind == "x":
                    act.wait_ge(quad_done, after(seg["e0"] - 1))
                if kind == "p":
                    act.wait_ge(x_turned, after(P_BASE - 1))

                def gen_part(r, j, seg=seg):
                    if seg["gen"]:
                        gates(seg, r, j)

                def body(at, tail=False, seg=seg, kind=kind):
                    if kind == "x" and at(0):
                        pair_up(seg, *at(0))
                    if at(1) and not tail:
                        gen_part(*at(1))
                    if kind == "x" and at(0):
                        turn_out(seg, *at(0))
                    if sqrt_on_act(seg) and at(1):
                        std(seg, *at(1))
                    if kind in ("z", "x") and at(2):
                        high(seg, *at(2))
                    if kind == "p" and at(2):
                        turn_out(seg, *at(2))
                    if kind == "p" and at(3):
                        gate_out(seg, *at(3))

                def quadrant(seg=seg, gen_part=gen_part, kind=kind):
                    gen_part(ROUNDS - 1, UNROLL - 1)
                    if not seg["contract"]:
                        return
                    if kind == "p":
                        act.wait_ge(centred, after(seg["m0"] + STEPS - 1))
                    if seg["e0"] == 4 * GROUPS_C:
                        pass
                    for e in range(seg["e0"], seg["e0"] + GROUPS_C):
                        act.wait_ge(contracted, after(e))
                        c0 = (e - seg["e0"]) * CG
                        a.activation(quad[:, :, c0:c0 + CG],
                                     banks[e % 2][:, :, :].rearrange("p b (c j) -> p j (b c)", j=P),
                                     ACT.Copy).then_inc(quad_done, 1)

                walk(act, seg, body, before_tail=quadrant)

        @block.vector
        def _(dve):
            v = nc.vector
            for s in (stats_done, rstd_done, normed, low_done, xt_done, made, added, scaled,
                      cols_spread, gate_spread):
                dve.sem_inc(s, START)
            chain = [0]

            def link(ins):
                chain[0] += 1
                ins.then_inc(prep_v, 1)
                dve.wait_ge(prep_v, chain[0])

            for h in range(2):
                v.memset(split[:, h, :, 0, 0:1], 1.0)
                v.memset(split[:, h, :, 1, 0:1], 0.0)
            v.memset(fold, 0.0)
            for n in range(2):
                v.memset(put_bias[n], 0.0)
            link(v.memset(bz_rows[:, :], 0.0))
            dve.wait_ge(idents, 2)
            v.tensor_copy(ident_b[:, :], ident[:, :])
            for h in range(2):
                last = v.tensor_copy(fold[:, h * C + 1:(h + 1) * C], ident[0:C, 1:C])
            link(last)
            for h in range(2):
                v.memset(fold[0:1, h * C + 1:(h + 1) * C], -1.0)
            dve.wait_ge(loaded, LOADED)
            for n in range(2):
                v.tensor_copy(put_bias[n][:, 0:1], norm_b[n])
            for n, s in enumerate(sets):
                last = v.tensor_scalar(scaled_w[n], raw[n], norm_w[s[5]], None, ALU.mult)
            link(last)
            PREPARED = chain[0]
            link(v.tensor_copy(bz_part[0], bz))
            link(v.tensor_tensor(bz_rest[0], bz, bz_part[0], ALU.subtract))
            link(v.tensor_copy(bz_part[1], bz_rest[0]))
            link(v.tensor_tensor(bz_rest[1], bz_rest[0], bz_part[1], ALU.subtract))
            link(v.tensor_copy(bz_part[2], bz_rest[1]))
            for n in range(3):
                v.tensor_copy(bz_rows[32 * n:32 * n + 1, :], bz_part[n][32 * n:32 * n + 1, :])
            dve.wait_ge(prep_pe, 1)
            for n, s in enumerate(sets):
                w = C if s[2] is None else 2 * C
                last = v.tensor_copy(s[0][:, 0, :], prep_ps[n][:, 0:w])
            v.tensor_copy(mask_ki[:, 0, :], ps_t[:, 0:2, :].rearrange("p a b -> p (a b)"))
            v.tensor_copy(mask_ki[:, 1, :], ps_t[:, 2:4, :].rearrange("p a b -> p (a b)"))
            link(v.memset(rstd[:, :, :], 0.0))
            for n, s in enumerate(sets):
                w = C if s[2] is None else 2 * C
                last = v.tensor_tensor(s[0][:, 1, :], prep_ps[n][:, 0:w], s[0][:, 0, :],
                                       ALU.subtract)
            last.then_inc(ready, 1)

            def spread(dst, src):
                return v.tensor_copy(dst.rearrange("p (j g r) -> p j g r", g=GROUPS, r=GRP),
                                     src.rearrange("p (g j r) -> p j g r", g=GROUPS, r=GRP))

            def spread_cols(seg, r, j):
                c = seg["cols0"] + number(r, j)
                dve.wait_ge(cols_landed, 16 * (c + 1))
                dve.wait_ge(projected, after(2 * (seg["k0"] + number(r, j) - 1) + 1))
                spread(chunk[:, 1], chunk[:, 0]).then_inc(cols_spread, 1)

            def spread_gate(seg, r, j):
                w = (seg["m0"] - P_BASE) // 2 + 2 * r + j // 2
                dve.wait_ge(gchunk_landed, 16 * (w + 1))
                dve.wait_ge(gate_mm, after(2 * w - 3))
                spread(gspread[j // 2], gchunk).then_inc(gate_spread, 1)

            def make(seg, r, j):
                layer, op, kind, half = seg["gen"]
                group, other = 2 * r + j // 2, j % 2
                for s in range(2):
                    dve.wait_ge(masked if layer == 0 else gated, after(2 * (seg["k0"] + number(r, j)) + s))
                    dst = operand[op][:, other, :, bass.ds(GRP * group + COLS * s, COLS)]
                    ps = banks[s][:, :, :].rearrange("p b (t c) -> p c (b t)", c=2 * C)
                    v.tensor_tensor(dst, ps[:, C:2 * C, :], sig[:, s].rearrange("p t c -> p c t"),
                                    ALU.mult).then_inc(made, 1)

            def statistics(seg, r, j):
                kind = seg["norm"][0]
                m, h = seg["m0"] + number(r, j), j % 2
                dve.wait_ge(centred, after(m - 2))
                if kind == "z":
                    dve.wait_ge(x_landed[j], landed(seg, r))
                if kind == "x":
                    dve.wait_ge(added, after(m - X_BASE))
                for c in range(0, COLS, 2):
                    if kind == "p":
                        src = quad[:, bass.ds(COLS * number(r, j) + c, 2), :]
                    else:
                        src = xin[:, j, c:c + 2, :]
                    last = v.bn_stats(stats[:, h, c:c + 2, :].rearrange("p a s -> p (a s)"),
                                      src.rearrange("p a c -> p c a"))
                last.then_inc(stats_done, 1)

            def add(seg, r, j):
                dve.wait_ge(mixed, after(seg["m0"] - X_BASE + number(r, j)))
                dve.wait_ge(x_landed[j], landed(seg, r))
                v.tensor_tensor(xin[:, j], xin[:, j], ps_w[:, :, :], ALU.add).then_inc(added, 1)

            def normalise(seg, r, j):
                m, h = seg["m0"] + number(r, j), j % 2
                dve.wait_ge(centred, after(m))
                if sqrt_on_act(seg):
                    dve.wait_ge(std_done, after(m))
                    v.reciprocal(rstd[:, h], var[:, h]).then_inc(rstd_done, 1)
                    dve.wait_ge(rstd_done, after(m))
                lo = 0 if seg["norm"][0] == "p" else 1
                v.tensor_tensor(xc[:, h, :, lo:], xc[:, h, :, lo:],
                                rstd[:, h].unsqueeze(2).broadcast_to([P, COLS, C - lo]),
                                ALU.mult).then_inc(normed, 1)

            def low(seg, r, j):
                m, h = seg["m0"] + number(r, j), j % 2
                dve.wait_ge(high_done, after(m))
                v.tensor_tensor(split[:, h, :, 1, 1:], xc[:, h, :, 1:], split[:, h, :, 0, 1:],
                                ALU.subtract).then_inc(low_done, 1)

            def xt_out(seg, r, j):
                m, h = seg["m0"] + number(r, j), j % 2
                dve.wait_ge(x_turned, after(m))
                if not (isinstance(m, int) and m < 4):
                    dve.wait_ge(xt_stored[j // 2], 16 * (seg["m0"] // 4 + r))
                v.tensor_copy(xt[:, j // 2, :, COLS * h:COLS * (h + 1), :].rearrange("p g j r -> p j g r"),
                              ps_x[:, h].rearrange("p j (g r) -> p j g r", r=GRP)).then_inc(xt_done, 1)

            def scale(seg, r, j):
                n, h = seg["m0"] - P_BASE + number(r, j), j % 2
                dve.wait_ge(gate_sig, after(n))
                dve.wait_ge(mixed, after(seg["m0"] - X_BASE + number(r, j)))
                v.tensor_tensor(gt[:, h], ps_w[:, :, :], gt[:, h], ALU.mult).then_inc(scaled, 1)

            for seg in SEGMENTS:
                kind = seg["norm"] and seg["norm"][0]
                if seg["e0"]:
                    dve.wait_ge(contracted, after(seg["e0"] - 1))
                    if kind == "p":
                        dve.wait_ge(quad_done, after(seg["e0"] - 1))

                def gen_part(r, j, seg=seg):
                    if seg["gen"]:
                        make(seg, r, j)

                def body(at, tail=False, seg=seg, kind=kind):
                    if seg["gen"] and seg["gen"][2] == "col" and at(0):
                        spread_cols(seg, *at(0))
                    if at(1) and not tail:
                        gen_part(*at(1))
                    if kind == "p" and at(1) and at(1)[1] % 2 == 0:
                        spread_gate(seg, *at(1))
                    if kind == "x" and at(0):
                        add(seg, *at(0))
                    if kind and at(0):
                        statistics(seg, *at(0))
                    if kind and at(1):
                        normalise(seg, *at(1))
                    if kind in ("z", "x"):
                        if at(2):
                            low(seg, *at(2))
                        if at(4):
                            xt_out(seg, *at(4))
                    if kind == "p" and at(3):
                        scale(seg, *at(3))

                walk(dve, seg, body, before_tail=lambda: gen_part(ROUNDS - 1, UNROLL - 1))

        @block.tensor
        def _(pe):
            mm = nc.tensor.matmul
            for s in (x_turned, projected, contracted, turned, mixed, gate_mm):
                pe.sem_inc(s, START)
            PREPARED = 4
            pe.wait_ge(prep_v, PREPARED)
            pe.wait_ge(loaded, LOADED)
            for n, s in enumerate(sets):
                w = C if s[2] is None else 2 * C
                dst = prep_ps[n][:, 0:w]
                mm(dst, fold, scaled_w[n], start=True, stop=False)
                mm(dst, put_bias[s[5]], raw[n], start=False, stop=s[3] is None)
                if s[3] is not None:
                    mm(dst, ident[0:1, :], bias_row[n], start=False, stop=True)
            for kh in range(HALVES):
                for ih in range(HALVES):
                    last = nc.tensor.transpose(ps_t[:, 2 * kh + ih, :],
                                               mask_kj[:, ih, kh * P:(kh + 1) * P], ident[:, :])
            last.then_inc(prep_pe, 1)
            pe.wait_ge(ready, 1)

            def project(seg, r, j, s):
                layer, op, kind, half = seg["gen"]
                k = seg["k0"] + number(r, j)
                if s == 0 and kind == "row":
                    pe.wait_ge(chunk_landed[j % 2], 16 * (seg["rows0"] // 2 + 2 * r + j // 2 + 1))
                if s == 0 and kind == "col":
                    pe.wait_ge(cols_spread, after(seg["cols0"] + number(r, j)))
                pe.wait_ge(made, after(2 * k + s - 2))
                w = (w_lhs if op == "lhs" else w_rhs)[layer]
                ps = banks[s][:, :, :].rearrange("p b (t c) -> p (b t) c", c=2 * C)
                for n in range(COLS):
                    vec = COLS * s + n
                    if kind == "row":
                        x_vec = chunk[:, j % 2].rearrange("p (j r) -> p j r", r=GRP)[:, :, vec]
                    else:
                        x_vec = chunk[:, 1].rearrange("p (j r) -> p j r", r=P)[:, vec, :]
                    mm(ps[:, n, :], x_vec, w[:, 0, :], start=True, stop=False)
                    last = mm(ps[:, n, :], x_vec, w[:, 1, :], start=False, stop=True)
                last.then_inc(projected, 1)

            def contract(seg):
                pe.wait_ge(made, after(2 * (seg["k0"] + CHUNKS) - 1))
                for e in range(seg["e0"], seg["e0"] + GROUPS_C):
                    pe.wait_ge(quad_done, after(e - 2))
                    for n in range(CG):
                        c = (e - seg["e0"]) * CG + n
                        dst = banks[e % 2][:, :, :].rearrange("p b (c j) -> p (b c) j", j=P)[:, n]
                        for kh in range(HALVES):
                            last = mm(dst, operand["lhs"][:, kh, c, :], operand["rhs"][:, kh, c, :],
                                      start=kh == 0, stop=kh == HALVES - 1)
                    last.then_inc(contracted, 1)

            def turn(seg, r, j):
                o = seg["m0"] - X_BASE + number(r, j)
                pe.wait_ge(turned_out, after(o - 1))
                if seg["norm"][0] == "x":
                    pe.wait_ge(paired, after(o))
                    src = opair[:, :, :]
                else:
                    pe.wait_ge(normed, after(seg["m0"] + number(r, j)))
                    src = xc[:, j % 2].rearrange("p (a b) c -> p a (b c)", b=2)
                for n in range(COLS // 2):
                    last = nc.tensor.transpose(ps_t[:, n, :], src[:, n, :], ident[:, :])
                last.then_inc(turned, 1)

            def mix(seg, r, j):
                o = seg["m0"] - X_BASE + number(r, j)
                pe.wait_ge(turned_out, after(o))
                if seg["norm"][0] == "x":
                    layer = 0
                    pe.wait_ge(added, after(o - 1))
                    mm(ps_w[:, :, :], ones_b[:, :],
                       bz_rows[:, :].unsqueeze(1).broadcast_to([P, COLS, C]), start=True, stop=True)
                else:
                    layer = 1
                    pe.wait_ge(scaled, after(o - 4 * STEPS - 1))
                for n in range(COLS // 2):
                    last = mm(ps_w[:, 2 * n:2 * n + 2, :], opair[:, n, :], w_out[layer][:, :],
                              start=layer == 1, stop=True,
                              skip_group_check=layer == 0)
                last.then_inc(mixed, 1)

            def turn_x(seg, r, j):
                m, h = seg["m0"] + number(r, j), j % 2
                pe.wait_ge(low_done, after(m))
                pe.wait_ge(xt_done, after(m - 2))
                for n in range(COLS):
                    last = nc.tensor.transpose(ps_x[:, h, n, :],
                                               split[:, h, n].rearrange("p a c -> p (a c)"),
                                               ident_b[:, :])
                last.then_inc(x_turned, 1)

            def gate_product(seg, r, j):
                n, h = seg["m0"] - P_BASE + number(r, j), j % 2
                if h == 0:
                    pe.wait_ge(gate_spread, after((seg["m0"] - P_BASE) // 2 + 2 * r + j // 2))
                pe.wait_ge(gate_sig, after(n - 1))
                g3 = ps_g.rearrange("p t c -> p (t c)").rearrange("p (t c) -> p t c", c=C)
                for c in range(COLS):
                    x_vec = gspread[j // 2].rearrange("p (j r) -> p j r", r=P)[:, COLS * h + c, :]
                    mm(g3[:, c, :], x_vec, w_gate[:, 0, :], start=True, stop=False)
                    last = mm(g3[:, c, :], x_vec, w_gate[:, 1, :], start=False, stop=True)
                last.then_inc(gate_mm, 1)

            for seg in SEGMENTS:
                kind = seg["norm"] and seg["norm"][0]
                if seg["gen"] and seg["e0"]:
                    pe.wait_ge(quad_done, after(seg["e0"] - 1))
                if kind == "p":
                    pe.wait_ge(xt_done, after(P_BASE - 1))

                def body(at, tail=False, seg=seg, kind=kind):
                    if kind == "x" and at(0):
                        turn(seg, *at(0))
                    if kind == "p" and at(2):
                        turn(seg, *at(2))
                    if seg["gen"] and at(0):
                        project(seg, *at(0), 0)
                    if kind == "x" and at(0):
                        mix(seg, *at(0))
                    if kind == "p" and at(2):
                        gate_product(seg, *at(2))
                    if seg["gen"] and at(0):
                        project(seg, *at(0), 1)
                    if kind == "p" and at(2):
                        mix(seg, *at(2))
                    if kind in ("z", "x") and at(3):
                        turn_x(seg, *at(3))

                walk(pe, seg, body,
                     before_tail=lambda: contract(seg) if seg["contract"] else None)


SQRT_STEPS = sum(STEPS for s in SEGMENTS if s["norm"] and s["norm"][0] == "z" and not s["gen"])
POW_BASE = SQRT_STEPS


def sqrt_on_act(seg):
    return bool(seg["norm"]) and seg["norm"][0] == "z" and not seg["gen"]


def landed(seg, r):
    return 16 * (seg["m0"] // 4 + r + 1)


_INS = ['x', 'L0_conv_mask', 'L0_conv_ln_w', 'L0_conv_ln_b', 'L0_conv_W_ap', 'L0_conv_b_ap',
        'L0_conv_W_ag', 'L0_conv_b_ag', 'L0_conv_W_bp', 'L0_conv_b_bp', 'L0_conv_W_bg',
        'L0_conv_b_bg', 'L0_conv_W_z', 'L0_conv_b_z', 'L1_conv_ln1_w', 'L1_conv_ln1_b',
        'L1_conv_left1', 'L1_conv_left2', 'L1_conv_right1', 'L1_conv_right2', 'L1_conv_ln2_w',
        'L1_conv_ln2_b', 'L1_conv_out_w', 'L1_conv_gate']
_OUTS = [((1, 256, 256, 64), 'float32')]


def kernel(**inputs):
    import numpy as _np
    import concourse.bacc as _bacc
    from concourse import mybir as _mybir
    from concourse.bass_utils import run_bass_kernel_spmd as _run

    nc = _bacc.Bacc("TRN2", target_bir_lowering=False, num_devices=1)
    arrays, args = {}, []
    for name in _INS:
        a = _np.ascontiguousarray(inputs[name])
        arrays[f"in_{name}_dram"] = a
        args.append(nc.dram_tensor(f"in_{name}_dram", a.shape, _mybir.dt.from_np(a.dtype), kind="ExternalInput").ap())
    for i, (shape, dtype) in enumerate(_OUTS):
        dt = _mybir.dt.from_np(_np.dtype(dtype))
        args.append(nc.dram_tensor(f"out_{i}_dram", shape, dt, kind="ExternalOutput").ap())
    triangle_layers(nc, *args)
    r = _run(nc, [arrays], core_ids=[0])
    got = tuple(r.results[0][f"out_{i}_dram"] for i in range(len(_OUTS)))
    return got[0]
```

```python
from contextlib import ExitStack

import concourse.bass as bass
from concourse import mybir

F32 = mybir.dt.float32
BF16 = mybir.dt.bfloat16
ALU = mybir.AluOpType
ACT = mybir.ActivationFunctionType

P = 128
C = 64
N = 256
HALVES = N // P
EPS = 1e-5
ROOT_C = 8.0
COLS = 8
STEPS = P // COLS
GRP = 16
GROUPS = P // GRP
CHUNKS = HALVES * GROUPS
UNROLL = 4
LAG = 4
CG = 8
START = 4


def after(step):
    return START + 1 + step


SEGMENTS = [
    dict(norm=("z", 0, 0), gen=None, contract=False),
    dict(norm=("z", 1, 0), gen=None, contract=False),
    dict(norm=("z", 0, 1), gen=(0, "rhs", "col", 0), contract=False),
    dict(norm=("z", 1, 1), gen=(0, "lhs", "row", 0), contract=True),
    dict(norm=("x", 0, 0), gen=(0, "lhs", "row", 1), contract=True),
    dict(norm=("x", 1, 0), gen=(0, "rhs", "col", 1), contract=True),
    dict(norm=("x", 1, 1), gen=(0, "lhs", "row", 0), contract=True),
    dict(norm=("x", 0, 1), gen=(1, "lhs", "row", 1), contract=False),
    dict(norm=None, gen=(1, "rhs", "row", 1), contract=True),
    dict(norm=("p", 1, 1), gen=(1, "rhs", "row", 0), contract=True),
    dict(norm=("p", 1, 0), gen=(1, "lhs", "row", 0), contract=True),
    dict(norm=("p", 0, 0), gen=(1, "rhs", "row", 1), contract=True),
    dict(norm=("p", 0, 1), gen=None, contract=False),
]
X_BASE = 4 * STEPS
P_BASE = 8 * STEPS
GROUPS_C = C // CG


def number_segments():
    m = k = e = rows = cols = 0
    for seg in SEGMENTS:
        seg.update(m0=m, k0=k, e0=e, rows0=rows, cols0=cols)
        m += STEPS if seg["norm"] else 0
        k += CHUNKS if seg["gen"] else 0
        rows += CHUNKS if seg["gen"] and seg["gen"][2] == "row" else 0
        cols += CHUNKS if seg["gen"] and seg["gen"][2] == "col" else 0
        e += GROUPS_C if seg["contract"] else 0


number_segments()


ROUNDS = STEPS // UNROLL


def walk(eng, seg, body, before_tail=None, ahead=False):
    def looking_back(r, j):
        def at(lag):
            over = (j - lag) // UNROLL
            r1, j1 = r + over, j - lag - UNROLL * over
            if isinstance(r, int) and not 0 <= r1 < ROUNDS:
                return None
            return r1, j1
        return at

    for j in range(UNROLL):
        body(looking_back(0, j))
    with eng.Fori(1, ROUNDS - ahead, 1) as r:
        for j in range(UNROLL):
            body(looking_back(r, j))
    if ahead:
        for j in range(UNROLL):
            body(looking_back(ROUNDS - 1, j))
    if before_tail:
        before_tail()
    if seg["norm"]:
        for j in range(LAG):
            body(looking_back(ROUNDS, j), tail=True)


def number(r, j):
    return UNROLL * r + j


def triangle_layers(nc, x, mask, ln_w, ln_b, W_ap, b_ap, W_ag, b_ag, W_bp, b_bp, W_bg, b_bg,
                    W_z, b_z, ln1_w, ln1_b, left1, left2, right1, right2, ln2_w, ln2_b, out_w,
                    gate, out):
    x3, out3 = x[0], out[0]
    xt_dram = [nc.dram_tensor(f"xt{n}", [HALVES, P, GROUPS, N, GRP], BF16).ap() for n in range(2)]
    x1_dram = nc.dram_tensor("x1", [N, N, C], F32).ap()

    with ExitStack() as ctx:
        def sb(name, shape, dt=F32):
            return ctx.enter_context(nc.sbuf_tensor(name, shape, dt))

        def sem(name):
            return ctx.enter_context(nc.semaphore(name))

        operand = {"lhs": sb("lhs", [P, HALVES, C, P]), "rhs": sb("rhs", [P, HALVES, C, P])}
        quad = sb("quad", [P, P, C])
        chunk = sb("chunk", [P, 2, P * GRP], BF16)
        sig = sb("sig", [P, 2, COLS, C])
        masks = sb("masks", [P, 2, HALVES, N])
        mask_kj, mask_ki = masks[:, 0], masks[:, 1]
        xin = sb("xin", [P, 4, COLS, C])
        xc = sb("xc", [P, 2, COLS, C])
        split = sb("split", [P, 2, COLS, 2, C], BF16)
        gt = split[:, :, :, :, :].bitcast(F32).rearrange("p b t a c -> p b t (a c)")
        xt = sb("xt", [P, 2, GROUPS, GRP, GRP], BF16)
        gchunk = xt[:, 0].rearrange("p g j r -> p (g j r)")
        gspread = [xt[:, 1].rearrange("p g j r -> p (g j r)"),
                   masks[:, :, :, :].rearrange("p a h n -> p (a h n)").bitcast(BF16)]
        opair = sb("opair", [P, COLS // 2, P])
        stats = sb("stats", [P, 2, COLS, 3])
        rstd = sb("rstd", [P, 2, COLS])
        var = sb("var", [P, 2, COLS])
        ident = sb("ident", [P, P])
        ident_b = sb("ident_b", [P, P], BF16)
        ones_b = sb("ones_b", [P, P], BF16)
        w_lhs = [sb(f"w_lhs{n}", [P, 2, 2 * C], BF16) for n in range(2)]
        w_rhs = [sb(f"w_rhs{n}", [P, 2, 2 * C], BF16) for n in range(2)]
        w_gate = sb("w_gate", [P, 2, C], BF16)
        w_out = [sb(f"w_out{n}", [P, P]) for n in range(2)]
        bz_rows = sb("bz_rows", [P, C], BF16)
        ln2 = sb("ln2", [P, 2])
        c_eps = sb("c_eps", [P, COLS])
        minus_half = sb("minus_half", [P, COLS])

        banks = [ctx.enter_context(nc.psum_tensor(f"bank{n}", [P, 2, 512], F32)) for n in range(2)]
        ps_t = ctx.enter_context(nc.psum_tensor("ps_t", [P, COLS // 2, P], F32))
        ps_w = ctx.enter_context(nc.psum_tensor("ps_w", [P, COLS, C], F32))
        ps_x = ctx.enter_context(nc.psum_tensor("ps_x", [P, 2, COLS, P], BF16))
        ps_g = [ps_x[:, n].bitcast(F32).rearrange("p t c -> p (t c)").rearrange(
            "p (t c) -> p t c", c=C) for n in range(2)]

        loaded = sem("loaded")
        zeroed = sem("zeroed")
        idents = sem("idents")
        prep_v, prep_pe = sem("prep_v"), sem("prep_pe")
        ready = sem("ready")
        x_landed = [sem(f"x_landed{n}") for n in range(4)]
        x_stored = [sem(f"x_stored{n}") for n in range(4)]
        chunk_landed = [sem(f"chunk_landed{n}") for n in range(2)]
        cols_landed, gchunk_landed = sem("cols_landed"), sem("gchunk_landed")
        cols_spread, gate_spread = sem("cols_spread"), sem("gate_spread")
        xt_stored = [sem(f"xt_stored{n}") for n in range(2)]
        stats_done, centred, std_done = sem("stats_done"), sem("centred"), sem("std_done")
        var_done, rstd_done, rooted = sem("var_done"), sem("rstd_done"), sem("rooted")
        normed, high_done, low_done = sem("normed"), sem("high_done"), sem("low_done")
        x_turned, xt_done = sem("x_turned"), sem("xt_done")
        projected, gated, masked, made = sem("projected"), sem("gated"), sem("masked"), sem("made")
        contracted, quad_done = sem("contracted"), sem("quad_done")
        paired, turned, turned_out = sem("paired"), sem("turned"), sem("turned_out")
        mixed, added = sem("mixed"), sem("added")
        gate_mm, gate_sig, scaled, summed = (sem("gate_mm"), sem("gate_sig"), sem("scaled"),
                                             sem("summed"))

        scratch = quad[:, :, :].rearrange("p j c -> p (j c)")
        at = [0]

        def temp(rows, width):
            at[0] += width
            return scratch[0:rows, at[0] - width:at[0]]

        sets = [
            (w_lhs[0], W_ag, W_ap, b_ag, b_ap, 0), (w_rhs[0], W_bg, W_bp, b_bg, b_bp, 0),
            (w_lhs[1], right1, right2, None, None, 1), (w_rhs[1], left1, left2, None, None, 1),
            (w_gate, gate, None, None, None, 1),
        ]
        raw = [temp(C, C if s[2] is None else 2 * C) for s in sets]
        scaled_w = [temp(C, C if s[2] is None else 2 * C) for s in sets]
        bias_row = [temp(1, 2 * C) if s[3] is not None else None for s in sets]
        norm_w = [temp(C, 1) for _ in range(2)]
        norm_b = [temp(C, 1) for _ in range(2)]
        fold = temp(C, P)
        put_bias = [temp(C, P) for _ in range(2)]
        bz = temp(P, C)
        bz_rest = [temp(P, C) for _ in range(2)]
        bz_part = [temp(P, C // 2).bitcast(BF16) for _ in range(3)]
        prep_ps = [banks[0][:, 0, 0:2 * C], banks[0][:, 1, 0:2 * C], banks[1][:, 0, 0:2 * C],
                   banks[1][:, 1, 0:2 * C], ps_w[:, 0:2, :].rearrange("p a c -> p (a c)")]

        def column(v):
            return v.rearrange("(c a) -> c a", a=1)

        def row(v):
            return v.rearrange("(a c) -> a c", a=1)

        loads = []
        for n, (dst, wg, wv, bg, bv, layer) in enumerate(sets):
            loads.append((raw[n][:, 0:C], wg))
            if wv is not None:
                loads.append((raw[n][:, C:2 * C], wv))
            if bg is not None:
                loads += [(bias_row[n][:, 0:C], row(bg)), (bias_row[n][:, C:2 * C], row(bv))]
        for n, (w, b) in enumerate([(ln_w, ln_b), (ln1_w, ln1_b)]):
            loads += [(norm_w[n], column(w)), (norm_b[n], column(b))]
        for n, v in enumerate((ln2_w, ln2_b)):
            loads += [(ln2[h * C:(h + 1) * C, n:n + 1], column(v)) for h in range(2)]
        loads.append((bz, row(b_z).broadcast_to([P, C])))
        loads.append((mask_kj[:, :, :], mask[0].rearrange("(h p) j -> p h j", p=P)))
        loads_diag = [(w_out[n][h * C:(h + 1) * C, h * C:(h + 1) * C], w)
                      for n, w in enumerate((W_z, out_w)) for h in range(2)]
        LOADED = 16 * (len(loads) + len(loads_diag))

        block = ctx.enter_context(nc.Block())

        @block.sync
        def _(sp):
            for s in x_stored:
                sp.sem_inc(s, 16)
            for dst, src in loads:
                sp.dma_start(dst, src).then_inc(loaded, 16)
            sp.wait_ge(zeroed, 1)
            for dst, src in loads_diag:
                sp.dma_start(dst, src).then_inc(loaded, 16)

            def load_x(seg, r, j):
                kind, rh, ch = seg["norm"]
                m = seg["m0"] + number(r, j)
                if kind != "p":
                    sp.wait_ge(centred, after(m - 4))
                if kind != "z":
                    sp.wait_ge(x_stored[j], 16 * (r + (seg["m0"] - X_BASE) // 4 + 1))
                src = (x1_dram if kind == "p" else x3)
                sp.dma_start(xin[:, j], src[rh * P:(rh + 1) * P, bass.ds(ch * P + COLS * number(r, j), COLS), :]
                             ).then_inc(x_landed[j], 16)

            def load_chunk(seg, r, j):
                layer, _, kind, half = seg["gen"]
                group, other = 2 * r + j // 2, j % 2
                buf = chunk[:, j % 2 if kind == "row" else 0]
                if kind == "col" and not (isinstance(r, int) and (r, j) == (0, 0)):
                    sp.wait_ge(cols_spread, after(seg["cols0"] + number(r, j) - 1))
                else:
                    sp.wait_ge(projected, after(2 * (seg["k0"] + number(r, j) - 2) + 1))
                    if isinstance(r, int) and (r, j) == (0, 0):
                        sp.wait_ge(cols_spread, after(seg["cols0"] - 1))
                if kind == "row":
                    src = xt_dram[layer][half, :, bass.ds(group, 1), other * P:(other + 1) * P, :]
                    dst = buf.rearrange("p (g j r) -> p g j r", g=1, r=GRP)
                else:
                    src = xt_dram[layer][other, :, :, bass.ds(half * P + GRP * group, GRP), :]
                    dst = buf.rearrange("p (g j r) -> p g j r", g=GROUPS, r=GRP)
                sp.dma_start(dst, src).then_inc(chunk_landed[j % 2] if kind == "row" else cols_landed,
                                                16)

            def load_gate(seg, r, j):
                _, rh, ch = seg["norm"]
                sp.wait_ge(gate_spread, after((seg["m0"] - P_BASE) // 2 + 2 * r + j // 2 - 1))
                sp.dma_start(gchunk.rearrange("p (g j r) -> p g j r", g=GROUPS, r=GRP),
                             xt_dram[1][rh, :, :, bass.ds(ch * P + COLS * number(r, j), GRP), :]
                             ).then_inc(gchunk_landed, 16)

            def store_x(seg, r, j):
                _, rh, ch = seg["norm"]
                sp.wait_ge(added, after(seg["m0"] + number(r, j) - X_BASE))
                sp.dma_start(x1_dram[rh * P:(rh + 1) * P, bass.ds(ch * P + COLS * number(r, j), COLS), :],
                             xin[:, j]).then_inc(x_stored[j], 16)

            def store_xt(seg, r, j):
                kind, rh, ch = seg["norm"]
                sp.wait_ge(xt_done, after(seg["m0"] + number(r, j)))
                sp.dma_start(xt_dram[kind == "x"][rh, :, :, bass.ds(ch * P + COLS * UNROLL * r + COLS * (j - 1), GRP), :],
                             xt[:, j // 2]).then_inc(xt_stored[j // 2], 16)

            def wait_stored(seg):
                pairs = min(seg["m0"], P_BASE) // 4
                if pairs:
                    for n in range(2):
                        sp.wait_ge(xt_stored[n], 16 * pairs)
                if seg["m0"] > X_BASE:
                    for n in range(4):
                        sp.wait_ge(x_stored[n], 16 + 16 * (seg["m0"] - X_BASE) // 4)

            def load_step(seg, r, j):
                if seg["gen"]:
                    load_chunk(seg, r, j)
                if seg["norm"] and seg["norm"][0] == "p" and j % 2 == 0:
                    load_gate(seg, r, j)
                if seg["norm"] and seg["norm"][0] != "p":
                    load_x(seg, r, j)

            load_step(SEGMENTS[0], 0, 0)
            for n, seg in enumerate(SEGMENTS):
                kind = seg["norm"] and seg["norm"][0]

                def body(at, tail=False, seg=seg, kind=kind):
                    if at(-1) and not tail:
                        load_step(seg, *at(-1))
                    if kind == "p" and at(2):
                        load_x(seg, *at(2))
                    if kind == "x" and at(2):
                        store_x(seg, *at(2))
                    if kind in ("z", "x") and at(4) and at(4)[1] % 2 == 1:
                        store_xt(seg, *at(4))

                def next_start():
                    if n + 1 < len(SEGMENTS):
                        wait_stored(seg)
                        load_step(SEGMENTS[n + 1], 0, 0)

                walk(sp, seg, body, before_tail=next_start, ahead=True)
                if n + 1 < len(SEGMENTS):
                    wait_stored(SEGMENTS[n + 1])
            for n in range(4):
                sp.wait_ge(x_stored[n], 16 + 16 * (3 * 4 * STEPS - X_BASE) // 4)

        @block.gpsimd
        def _(pool):
            g = nc.gpsimd
            for s in (centred, masked, summed, var_done, rooted):
                pool.sem_inc(s, START)
            g.memset(ident[:, :], 0.0).then_inc(idents, 1)
            for n in range(2):
                last = g.memset(w_out[n][:, :], 0.0)
            last.then_inc(zeroed, 1)
            g.memset(minus_half[:, :], -0.5)
            g.memset(c_eps[:, :], C * EPS)
            g.memset(ones_b[:, :], 1.0)
            pool.wait_ge(idents, 1)
            g.affine_select(out=ident[:, :], in_=ident[:, :], compare_op=ALU.not_equal, fill=1.0,
                            base=0, pattern=[[-1, P]], channel_multiplier=1).then_inc(idents, 1)
            pool.wait_ge(ready, 1)

            def mask_gate(seg, r, j, s):
                layer, op, kind, half = seg["gen"]
                group, other = 2 * r + j // 2, j % 2
                table = mask_ki if kind == "row" else mask_kj
                pool.wait_ge(gated, after(2 * (seg["k0"] + number(r, j)) + s))
                m8 = table[:, other, bass.ds(half * P + GRP * group + COLS * s, COLS)].unsqueeze(2)
                g.tensor_tensor(sig[:, s], sig[:, s], m8.broadcast_to([P, COLS, C]),
                                ALU.mult).then_inc(masked, 1)

            def centre(seg, r, j):
                m, h = seg["m0"] + number(r, j), j % 2
                pool.wait_ge(stats_done, after(m))
                pool.wait_ge(low_done, after(m - 2))
                g.tensor_tensor(xc[:, h, :, 1:], xin[:, j, :, 1:],
                                stats[:, h, :, 1:2].broadcast_to([P, COLS, C - 1]),
                                ALU.subtract).then_inc(centred, 1)

            def root(seg, r, j):
                m, h = seg["m0"] + number(r, j), j % 2
                pool.wait_ge(normed, after(m - 2))
                pool.wait_ge(stats_done, after(m))
                g.tensor_tensor(var[:, h], stats[:, h, :, 2], c_eps[:, :], ALU.add
                                ).then_inc(var_done, 1)
                pool.wait_ge(var_done, after(m - SQRT_STEPS))
                g.tensor_tensor(rstd[:, h], var[:, h], minus_half[:, :], ALU.pow
                                ).then_inc(rooted, 1)

            def add_residual(seg, r, j):
                m, h = seg["m0"] + number(r, j), j % 2
                pool.wait_ge(scaled, after(m - P_BASE))
                pool.wait_ge(x_landed[j], landed(seg, r))
                g.tensor_tensor(xin[:, j], xin[:, j], gt[:, h], ALU.add).then_inc(summed, 1)

            for seg in SEGMENTS:
                masks_gates = seg["gen"] and seg["gen"][0] == 0

                def body(at, tail=False, seg=seg, masks_gates=masks_gates):
                    if seg["norm"] and seg["norm"][0] == "p" and at(4):
                        add_residual(seg, *at(4))
                    if masks_gates and at(1) and not tail:
                        mask_gate(seg, *at(1), 1)
                    if seg["norm"] and at(1) and not centre_on_vector(seg):
                        centre(seg, *at(1))
                    if seg["norm"] and at(1) and not sqrt_on_act(seg):
                        root(seg, *at(1))
                    if masks_gates and at(0):
                        mask_gate(seg, *at(0), 0)

                def last_mask():
                    if masks_gates:
                        mask_gate(seg, ROUNDS - 1, UNROLL - 1, 1)

                walk(pool, seg, body, before_tail=last_mask)

        @block.scalar
        def _(act):
            a = nc.scalar
            for s in (std_done, high_done, xt_done, gated, quad_done, paired, turned_out, gate_sig):
                act.sem_inc(s, START)
            act.wait_ge(ready, 1)

            def gates(seg, r, j, s):
                n = 2 * (seg["k0"] + number(r, j)) + s
                act.wait_ge(projected, after(n))
                act.wait_ge(made, after(n - 2))
                v = banks[s][:, :, :].rearrange("p b (t c) -> p (b t) c", c=2 * C)
                a.activation(sig[:, s], v[:, :, 0:C], ACT.Sigmoid).then_inc(gated, 1)

            def std(seg, r, j):
                m, h = seg["m0"] + number(r, j), j % 2
                act.wait_ge(stats_done, after(m))
                act.wait_ge(normed, after(m - 2))
                a.activation(var[:, h], stats[:, h, :, 2], ACT.Sqrt, bias=c_eps[:, 0:1]).then_inc(std_done, 1)

            def high(seg, r, j):
                m, h = seg["m0"] + number(r, j), j % 2
                act.wait_ge(normed, after(m))
                act.wait_ge(x_turned, after(m - 2))
                a.activation(split[:, h, :, 0, 1:], xc[:, h, :, 1:], ACT.Copy
                             ).then_inc(high_done, 1)

            def pair_up(seg, r, j):
                o = seg["m0"] - X_BASE + number(r, j)
                act.wait_ge(mixed, after(o - 1))
                a.activation(opair[:, :, :].rearrange("p a (b c) -> p (a b) c", c=C),
                             quad[:, bass.ds(COLS * number(r, j), COLS), :], ACT.Copy).then_inc(paired, 1)

            def turn_out(seg, r, j):
                o = seg["m0"] - X_BASE + number(r, j)
                act.wait_ge(turned, after(o))
                if seg["norm"][0] == "x":
                    a.activation(opair[:, :, :], ps_t[:, :, :], ACT.Copy).then_inc(turned_out, 1)
                else:
                    act.wait_ge(mixed, after(o - 1))
                    a.activation(opair[:, :, :], ps_t[:, :, :], ACT.Identity, scale=ln2[:, 0:1],
                                 bias=ln2[:, 1:2]).then_inc(turned_out, 1)

            def xt_out(seg, r, j):
                m, h = seg["m0"] + number(r, j), j % 2
                act.wait_ge(x_turned, after(m))
                if not (isinstance(m, int) and m < 4):
                    act.wait_ge(xt_stored[j // 2], 16 * (seg["m0"] // 4 + r))
                a.activation(xt[:, j // 2, :, COLS * h:COLS * (h + 1), :].rearrange("p g j r -> p j g r"),
                              ps_x[:, h].rearrange("p j (g r) -> p j g r", r=GRP), ACT.Copy).then_inc(xt_done, 1)

            def store_out(seg, r, j):
                _, rh, ch = seg["norm"]
                act.wait_ge(summed, after(seg["m0"] + number(r, j) - P_BASE))
                act.dma_start(out3[rh * P:(rh + 1) * P, bass.ds(ch * P + COLS * number(r, j), COLS), :],
                              xin[:, j]).then_inc(x_stored[j], 16)

            def gate_out(seg, r, j):
                n, h = seg["m0"] - P_BASE + number(r, j), j % 2
                act.wait_ge(gate_mm, after(n))
                act.wait_ge(summed, after(n - 2))
                a.activation(gt[:, h], ps_g[h], ACT.Sigmoid).then_inc(gate_sig, 1)

            for seg in SEGMENTS:
                kind = seg["norm"] and seg["norm"][0]
                if kind == "x":
                    act.wait_ge(quad_done, after(seg["e0"] - 1))
                if kind == "p":
                    act.wait_ge(x_turned, after(P_BASE - 1))

                def body(at, tail=False, seg=seg, kind=kind):
                    if kind == "x" and at(0):
                        pair_up(seg, *at(0))
                    if seg["gen"] and at(1) and not tail:
                        gates(seg, *at(1), 1)
                    if kind == "p" and at(3):
                        gate_out(seg, *at(3))
                    if kind in ("z", "x") and at(2):
                        high(seg, *at(2))
                    if kind in ("z", "x") and at(3):
                        xt_out(seg, *at(3))
                    if sqrt_on_act(seg) and at(1):
                        std(seg, *at(1))
                    if kind == "x" and at(0):
                        turn_out(seg, *at(0))
                    if kind == "p" and at(2):
                        turn_out(seg, *at(2))
                    if seg["gen"] and at(0):
                        gates(seg, *at(0), 0)
                    if kind == "p" and at(4):
                        store_out(seg, *at(4))

                def quadrant(seg=seg, kind=kind):
                    if seg["gen"]:
                        gates(seg, ROUNDS - 1, UNROLL - 1, 1)
                    if not seg["contract"]:
                        return
                    if kind == "p":
                        act.wait_ge(centred, after(seg["m0"] + STEPS - 1))
                    for e in range(seg["e0"], seg["e0"] + GROUPS_C):
                        act.wait_ge(contracted, after(e))
                        c0 = (e - seg["e0"]) * CG
                        a.activation(quad[:, :, c0:c0 + CG],
                                     banks[e % 2][:, :, :].rearrange("p b (c j) -> p j (b c)", j=P),
                                     ACT.Copy).then_inc(quad_done, 1)

                walk(act, seg, body, before_tail=quadrant)

        @block.vector
        def _(dve):
            v = nc.vector
            for s in (stats_done, rstd_done, normed, low_done, made, added, scaled,
                      cols_spread, gate_spread):
                dve.sem_inc(s, START)
            chain = [0]

            def link(ins):
                chain[0] += 1
                ins.then_inc(prep_v, 1)
                dve.wait_ge(prep_v, chain[0])

            for h in range(2):
                v.memset(split[:, h, :, 0, 0:1], 1.0)
                v.memset(split[:, h, :, 1, 0:1], 0.0)
            v.memset(fold, 0.0)
            for n in range(2):
                v.memset(put_bias[n], 0.0)
            link(v.memset(bz_rows[:, :], 0.0))
            dve.wait_ge(idents, 2)
            v.tensor_copy(ident_b[:, :], ident[:, :])
            for h in range(2):
                last = v.tensor_scalar(fold[:, h * C + 1:(h + 1) * C], ident[0:C, 1:C], ROOT_C, None,
                                       ALU.mult)
            link(last)
            for h in range(2):
                v.memset(fold[0:1, h * C + 1:(h + 1) * C], -ROOT_C)
            dve.wait_ge(loaded, LOADED)
            for n in range(2):
                v.tensor_copy(put_bias[n][:, 0:1], norm_b[n])
            for n, s in enumerate(sets):
                last = v.tensor_scalar(scaled_w[n], raw[n], norm_w[s[5]], None, ALU.mult)
            link(last)
            PREPARED = chain[0]
            link(v.tensor_copy(bz_part[0], bz))
            link(v.tensor_tensor(bz_rest[0], bz, bz_part[0], ALU.subtract))
            link(v.tensor_copy(bz_part[1], bz_rest[0]))
            link(v.tensor_tensor(bz_rest[1], bz_rest[0], bz_part[1], ALU.subtract))
            link(v.tensor_copy(bz_part[2], bz_rest[1]))
            for n in range(3):
                v.tensor_copy(bz_rows[32 * n:32 * n + 1, :], bz_part[n][32 * n:32 * n + 1, :])
            dve.wait_ge(prep_pe, 1)
            for n, s in enumerate(sets):
                w = C if s[2] is None else 2 * C
                last = v.tensor_copy(s[0][:, 0, :], prep_ps[n][:, 0:w])
            v.tensor_copy(mask_ki[:, 0, :], ps_t[:, 0:2, :].rearrange("p a b -> p (a b)"))
            v.tensor_copy(mask_ki[:, 1, :], ps_t[:, 2:4, :].rearrange("p a b -> p (a b)"))
            v.tensor_scalar(ln2[:, 0:1], ln2[:, 0:1], ROOT_C, None, ALU.mult)
            link(v.memset(rstd[:, :, :], 0.0))
            for n, s in enumerate(sets):
                w = C if s[2] is None else 2 * C
                last = v.tensor_tensor(s[0][:, 1, :], prep_ps[n][:, 0:w], s[0][:, 0, :],
                                       ALU.subtract)
            last.then_inc(ready, 1)

            def spread(dst, src):
                return v.tensor_copy(dst.rearrange("p (j g r) -> p j g r", g=GROUPS, r=GRP),
                                     src.rearrange("p (g j r) -> p j g r", g=GROUPS, r=GRP))

            def spread_cols(seg, r, j):
                c = seg["cols0"] + number(r, j)
                dve.wait_ge(cols_landed, 16 * (c + 1))
                dve.wait_ge(projected, after(2 * (seg["k0"] + number(r, j) - 1) + 1))
                spread(chunk[:, 1], chunk[:, 0]).then_inc(cols_spread, 1)

            def spread_gate(seg, r, j):
                w = (seg["m0"] - P_BASE) // 2 + 2 * r + j // 2
                dve.wait_ge(gchunk_landed, 16 * (w + 1))
                dve.wait_ge(gate_mm, after(2 * w - 3))
                spread(gspread[j // 2], gchunk).then_inc(gate_spread, 1)

            def make(seg, r, j, s):
                layer, op, kind, half = seg["gen"]
                group, other = 2 * r + j // 2, j % 2
                dve.wait_ge(masked if layer == 0 else gated, after(2 * (seg["k0"] + number(r, j)) + s))
                dst = operand[op][:, other, :, bass.ds(GRP * group + COLS * s, COLS)]
                ps = banks[s][:, :, :].rearrange("p b (t c) -> p c (b t)", c=2 * C)
                v.tensor_tensor(dst, ps[:, C:2 * C, :], sig[:, s].rearrange("p t c -> p c t"),
                                ALU.mult).then_inc(made, 1)

            def statistics(seg, r, j):
                kind = seg["norm"][0]
                m, h = seg["m0"] + number(r, j), j % 2
                dve.wait_ge(centred, after(m - 2))
                if kind == "z":
                    dve.wait_ge(x_landed[j], landed(seg, r))
                if kind == "x":
                    dve.wait_ge(added, after(m - X_BASE))
                for c in range(0, COLS, 2):
                    if kind == "p":
                        src = quad[:, bass.ds(COLS * number(r, j) + c, 2), :]
                    else:
                        src = xin[:, j, c:c + 2, :]
                    last = v.bn_stats(stats[:, h, c:c + 2, :].rearrange("p a s -> p (a s)"),
                                      src.rearrange("p a c -> p c a"))
                last.then_inc(stats_done, 1)

            def add(seg, r, j):
                dve.wait_ge(mixed, after(seg["m0"] - X_BASE + number(r, j)))
                dve.wait_ge(x_landed[j], landed(seg, r))
                v.tensor_tensor(xin[:, j], xin[:, j], ps_w[:, :, :], ALU.add).then_inc(added, 1)

            def centre(seg, r, j):
                m, h = seg["m0"] + number(r, j), j % 2
                if seg["norm"][0] == "p":
                    dve.wait_ge(turned, after(m - X_BASE - 2))
                    src, lo = quad[:, bass.ds(COLS * number(r, j), COLS), :], 0
                else:
                    dve.wait_ge(low_done, after(m - 2))
                    src, lo = xin[:, j], 1
                dve.wait_ge(stats_done, after(m))
                v.tensor_tensor(xc[:, h, :, lo:], src[:, :, lo:],
                                stats[:, h, :, 1:2].broadcast_to([P, COLS, C - lo]),
                                ALU.subtract).then_inc(centred, 1)

            def normalise(seg, r, j):
                m, h = seg["m0"] + number(r, j), j % 2
                dve.wait_ge(centred, after(m))
                if not sqrt_on_act(seg):
                    dve.wait_ge(rooted, after(m - SQRT_STEPS))
                if sqrt_on_act(seg):
                    dve.wait_ge(std_done, after(m))
                    v.reciprocal(rstd[:, h], var[:, h]).then_inc(rstd_done, 1)
                    dve.wait_ge(rstd_done, after(m))
                lo = 0 if seg["norm"][0] == "p" else 1
                v.tensor_tensor(xc[:, h, :, lo:], xc[:, h, :, lo:],
                                rstd[:, h].unsqueeze(2).broadcast_to([P, COLS, C - lo]),
                                ALU.mult).then_inc(normed, 1)

            def low(seg, r, j):
                m, h = seg["m0"] + number(r, j), j % 2
                dve.wait_ge(high_done, after(m))
                v.tensor_tensor(split[:, h, :, 1, 1:], xc[:, h, :, 1:], split[:, h, :, 0, 1:],
                                ALU.subtract).then_inc(low_done, 1)

            def scale(seg, r, j):
                n, h = seg["m0"] - P_BASE + number(r, j), j % 2
                dve.wait_ge(gate_sig, after(n))
                dve.wait_ge(mixed, after(seg["m0"] - X_BASE + number(r, j)))
                v.tensor_tensor(gt[:, h], ps_w[:, :, :], gt[:, h], ALU.mult).then_inc(scaled, 1)

            for seg in SEGMENTS:
                kind = seg["norm"] and seg["norm"][0]
                if seg["e0"]:
                    dve.wait_ge(contracted, after(seg["e0"] - 1))
                    if kind == "p":
                        dve.wait_ge(quad_done, after(seg["e0"] - 1))

                def body(at, tail=False, seg=seg, kind=kind):
                    if seg["gen"] and seg["gen"][2] == "col" and at(0):
                        spread_cols(seg, *at(0))
                    if kind == "x" and at(1):
                        statistics(seg, *at(1))
                    if kind in ("z", "p") and at(0):
                        statistics(seg, *at(0))
                    if seg["gen"] and at(1) and not tail:
                        make(seg, *at(1), 1)
                    if kind and centre_on_vector(seg) and at(1):
                        centre(seg, *at(1))
                    if kind in ("z", "x") and at(2):
                        low(seg, *at(2))
                    if kind == "x" and at(0):
                        add(seg, *at(0))
                    if kind == "p" and at(3):
                        scale(seg, *at(3))
                    if kind and at(1):
                        normalise(seg, *at(1))
                    if seg["gen"] and at(0):
                        make(seg, *at(0), 0)
                    if kind == "p" and at(1) and at(1)[1] % 2 == 0:
                        spread_gate(seg, *at(1))

                def last_make():
                    if seg["gen"]:
                        make(seg, ROUNDS - 1, UNROLL - 1, 1)

                walk(dve, seg, body, before_tail=last_make)

        @block.tensor
        def _(pe):
            mm = nc.tensor.matmul
            for s in (x_turned, projected, contracted, turned, mixed, gate_mm):
                pe.sem_inc(s, START)
            PREPARED = 4
            pe.wait_ge(prep_v, PREPARED)
            pe.wait_ge(loaded, LOADED)
            for n, s in enumerate(sets):
                w = C if s[2] is None else 2 * C
                dst = prep_ps[n][:, 0:w]
                mm(dst, fold, scaled_w[n], start=True, stop=False)
                mm(dst, put_bias[s[5]], raw[n], start=False, stop=s[3] is None)
                if s[3] is not None:
                    mm(dst, ident[0:1, :], bias_row[n], start=False, stop=True)
            for kh in range(HALVES):
                for ih in range(HALVES):
                    last = nc.tensor.transpose(ps_t[:, 2 * kh + ih, :],
                                               mask_kj[:, ih, kh * P:(kh + 1) * P], ident[:, :])
            last.then_inc(prep_pe, 1)
            pe.wait_ge(ready, 1)

            def project(seg, r, j, s):
                layer, op, kind, half = seg["gen"]
                k = seg["k0"] + number(r, j)
                if s == 0 and kind == "row":
                    pe.wait_ge(chunk_landed[j % 2], 16 * (seg["rows0"] // 2 + 2 * r + j // 2 + 1))
                if s == 0 and kind == "col":
                    pe.wait_ge(cols_spread, after(seg["cols0"] + number(r, j)))
                pe.wait_ge(made, after(2 * k + s - 2))
                w = (w_lhs if op == "lhs" else w_rhs)[layer]
                ps = banks[s][:, :, :].rearrange("p b (t c) -> p (b t) c", c=2 * C)
                for n in range(COLS):
                    vec = COLS * s + n
                    if kind == "row":
                        x_vec = chunk[:, j % 2].rearrange("p (j r) -> p j r", r=GRP)[:, :, vec]
                    else:
                        x_vec = chunk[:, 1].rearrange("p (j r) -> p j r", r=P)[:, vec, :]
                    mm(ps[:, n, :], x_vec, w[:, 0, :], start=True, stop=False)
                    last = mm(ps[:, n, :], x_vec, w[:, 1, :], start=False, stop=True)
                last.then_inc(projected, 1)

            def contract(seg):
                pe.wait_ge(made, after(2 * (seg["k0"] + CHUNKS) - 1))
                for e in range(seg["e0"], seg["e0"] + GROUPS_C):
                    pe.wait_ge(quad_done, after(e - 2))
                    for n in range(CG):
                        c = (e - seg["e0"]) * CG + n
                        dst = banks[e % 2][:, :, :].rearrange("p b (c j) -> p (b c) j", j=P)[:, n]
                        for kh in range(HALVES):
                            last = mm(dst, operand["lhs"][:, kh, c, :], operand["rhs"][:, kh, c, :],
                                      start=kh == 0, stop=kh == HALVES - 1)
                    last.then_inc(contracted, 1)

            def turn(seg, r, j):
                o = seg["m0"] - X_BASE + number(r, j)
                pe.wait_ge(turned_out, after(o - 1))
                if seg["norm"][0] == "x":
                    pe.wait_ge(paired, after(o))
                    src = opair[:, :, :]
                else:
                    pe.wait_ge(normed, after(seg["m0"] + number(r, j)))
                    src = xc[:, j % 2].rearrange("p (a b) c -> p a (b c)", b=2)
                for n in range(COLS // 2):
                    last = nc.tensor.transpose(ps_t[:, n, :], src[:, n, :], ident[:, :])
                last.then_inc(turned, 1)

            def mix(seg, r, j):
                o = seg["m0"] - X_BASE + number(r, j)
                pe.wait_ge(turned_out, after(o))
                if seg["norm"][0] == "x":
                    layer = 0
                    pe.wait_ge(added, after(o - 1))
                    mm(ps_w[:, :, :], ones_b[:, :],
                       bz_rows[:, :].unsqueeze(1).broadcast_to([P, COLS, C]), start=True, stop=True)
                else:
                    layer = 1
                    pe.wait_ge(scaled, after(o - 4 * STEPS - 1))
                for n in range(COLS // 2):
                    last = mm(ps_w[:, 2 * n:2 * n + 2, :], opair[:, n, :], w_out[layer][:, :],
                              start=layer == 1, stop=True,
                              skip_group_check=layer == 0)
                last.then_inc(mixed, 1)

            def turn_x(seg, r, j):
                m, h = seg["m0"] + number(r, j), j % 2
                pe.wait_ge(low_done, after(m))
                pe.wait_ge(xt_done, after(m - 2))
                for n in range(COLS):
                    last = nc.tensor.transpose(ps_x[:, h, n, :],
                                               split[:, h, n].rearrange("p a c -> p (a c)"),
                                               ident_b[:, :])
                last.then_inc(x_turned, 1)

            def gate_product(seg, r, j):
                n, h = seg["m0"] - P_BASE + number(r, j), j % 2
                if h == 0:
                    pe.wait_ge(gate_spread, after((seg["m0"] - P_BASE) // 2 + 2 * r + j // 2))
                pe.wait_ge(gate_sig, after(n - 2))
                for c in range(COLS):
                    x_vec = gspread[j // 2].rearrange("p (j r) -> p j r", r=P)[:, COLS * h + c, :]
                    mm(ps_g[h][:, c, :], x_vec, w_gate[:, 0, :], start=True, stop=False)
                    last = mm(ps_g[h][:, c, :], x_vec, w_gate[:, 1, :], start=False, stop=True)
                last.then_inc(gate_mm, 1)

            for seg in SEGMENTS:
                kind = seg["norm"] and seg["norm"][0]
                if seg["gen"] and seg["e0"]:
                    pe.wait_ge(quad_done, after(seg["e0"] - 1))
                if kind == "p":
                    pe.wait_ge(xt_done, after(P_BASE - 1))

                def body(at, tail=False, seg=seg, kind=kind):
                    if kind == "x" and at(0):
                        turn(seg, *at(0))
                    if kind == "p" and at(2):
                        turn(seg, *at(2))
                    if seg["gen"] and at(0):
                        project(seg, *at(0), 0)
                    if kind == "x" and at(0):
                        mix(seg, *at(0))
                    if kind == "p" and at(2):
                        gate_product(seg, *at(2))
                    if seg["gen"] and at(0):
                        project(seg, *at(0), 1)
                    if kind == "p" and at(2):
                        mix(seg, *at(2))
                    if kind in ("z", "x") and at(2):
                        turn_x(seg, *at(2))

                walk(pe, seg, body,
                     before_tail=lambda: contract(seg) if seg["contract"] else None)


SQRT_STEPS = sum(STEPS for s in SEGMENTS if s["norm"] and s["norm"][0] == "z" and not s["gen"])


def sqrt_on_act(seg):
    return bool(seg["norm"]) and seg["norm"][0] == "z" and not seg["gen"]


def centre_on_vector(seg):
    return bool(seg["norm"]) and not sqrt_on_act(seg)


def landed(seg, r):
    return 16 * (seg["m0"] // 4 + r + 1)


_INS = ['x', 'L0_conv_mask', 'L0_conv_ln_w', 'L0_conv_ln_b', 'L0_conv_W_ap', 'L0_conv_b_ap',
        'L0_conv_W_ag', 'L0_conv_b_ag', 'L0_conv_W_bp', 'L0_conv_b_bp', 'L0_conv_W_bg',
        'L0_conv_b_bg', 'L0_conv_W_z', 'L0_conv_b_z', 'L1_conv_ln1_w', 'L1_conv_ln1_b',
        'L1_conv_left1', 'L1_conv_left2', 'L1_conv_right1', 'L1_conv_right2', 'L1_conv_ln2_w',
        'L1_conv_ln2_b', 'L1_conv_out_w', 'L1_conv_gate']
_OUTS = [((1, 256, 256, 64), 'float32')]


def kernel(**inputs):
    import numpy as _np
    import concourse.bacc as _bacc
    from concourse import mybir as _mybir
    from concourse.bass_utils import run_bass_kernel_spmd as _run

    nc = _bacc.Bacc("TRN2", target_bir_lowering=False, num_devices=1)
    arrays, args = {}, []
    for name in _INS:
        a = _np.ascontiguousarray(inputs[name])
        arrays[f"in_{name}_dram"] = a
        args.append(nc.dram_tensor(f"in_{name}_dram", a.shape, _mybir.dt.from_np(a.dtype), kind="ExternalInput").ap())
    for i, (shape, dtype) in enumerate(_OUTS):
        dt = _mybir.dt.from_np(_np.dtype(dtype))
        args.append(nc.dram_tensor(f"out_{i}_dram", shape, dt, kind="ExternalOutput").ap())
    triangle_layers(nc, *args)
    r = _run(nc, [arrays], core_ids=[0])
    got = tuple(r.results[0][f"out_{i}_dram"] for i in range(len(_OUTS)))
    return got[0]
```

```python
from contextlib import ExitStack

import concourse.bass as bass
from concourse import mybir

F32 = mybir.dt.float32
BF16 = mybir.dt.bfloat16
ALU = mybir.AluOpType
ACT = mybir.ActivationFunctionType

P = 128
C = 64
N = 256
HALVES = N // P
EPS = 1e-5
ROOT_C = C ** 0.5
COLS = 8
STEPS = P // COLS
GRP = 16
GROUPS = P // GRP
CHUNKS = HALVES * GROUPS
UNROLL = 4
LAG = 4
CG = 8
START = 4


def after(step):
    return START + 1 + step


SEGMENTS = [
    dict(norm=("z", 0, 0), gen=None, contract=False),
    dict(norm=("z", 1, 0), gen=None, contract=False, joined=4),
    dict(norm=("z", 0, 1), gen=(0, "rhs", "col", 0), contract=False),
    dict(norm=("z", 1, 1), gen=(0, "lhs", "row", 0), contract=True),
    dict(norm=("x", 0, 0), gen=(0, "lhs", "row", 1), contract=True),
    dict(norm=("x", 1, 0), gen=(0, "rhs", "col", 1), contract=True),
    dict(norm=("x", 1, 1), gen=(0, "lhs", "row", 0), contract=True),
    dict(norm=("x", 0, 1), gen=(1, "lhs", "row", 1), contract=False),
    dict(norm=None, gen=(1, "rhs", "row", 1), contract=True, joined=2),
    dict(norm=("p", 1, 1), gen=(1, "rhs", "row", 0), contract=True),
    dict(norm=("p", 1, 0), gen=(1, "lhs", "row", 0), contract=True),
    dict(norm=("p", 0, 0), gen=(1, "rhs", "row", 1), contract=True),
    dict(norm=("p", 0, 1), gen=None, contract=False),
]
X_BASE = 4 * STEPS
P_BASE = 8 * STEPS
GROUPS_C = C // CG


def number_segments():
    m = k = e = rows = cols = 0
    for seg in SEGMENTS:
        seg.update(m0=m, k0=k, e0=e, rows0=rows, cols0=cols, buffers=2 if seg["norm"] else 4)
        m += STEPS if seg["norm"] else 0
        k += CHUNKS if seg["gen"] else 0
        rows += CHUNKS // seg["buffers"] if seg["gen"] and seg["gen"][2] == "row" else 0
        cols += CHUNKS if seg["gen"] and seg["gen"][2] == "col" else 0
        e += GROUPS_C if seg["contract"] else 0


number_segments()


ROUNDS = STEPS // UNROLL
FIRST_GEN = next(seg for seg in SEGMENTS if seg["gen"])


def hands_on(seg):
    return any("joined" in follower for one, follower in zip(SEGMENTS, SEGMENTS[1:])
               if one is seg)


def walk(eng, seg, body, finish, carried=None, ahead=False, hand_on=None):
    def looking_back(r, j):
        def at(lag):
            over = (j - lag) // UNROLL
            r1, j1 = r + over, j - lag - UNROLL * over
            if isinstance(r, int) and not 0 <= r1 < ROUNDS:
                return None
            return r1, j1
        return at

    for j in range(UNROLL):
        if carried and j < seg["joined"]:
            carried(j)
        if carried and j == seg["joined"]:
            for n in range(j, LAG):
                carried(n)
        body(looking_back(0, j))
    with eng.Fori(1, ROUNDS - ahead, 1) as r:
        for j in range(UNROLL):
            body(looking_back(r, j))
    if ahead:
        for j in range(UNROLL):
            body(looking_back(ROUNDS - 1, j))

    def tail(j):
        if seg["norm"] and j < LAG:
            body(looking_back(ROUNDS, j), tail=True)

    if hands_on(seg) if hand_on is None else hand_on:
        finish(lambda j: None)
        return tail
    finish(tail)


def first_round(at):
    return isinstance(at(0)[0], int) and at(0)[0] == 0


def number(r, j):
    return UNROLL * r + j


def triangle_layers(nc, x, mask, ln_w, ln_b, W_ap, b_ap, W_ag, b_ag, W_bp, b_bp, W_bg, b_bg,
                    W_z, b_z, ln1_w, ln1_b, left1, left2, right1, right2, ln2_w, ln2_b, out_w,
                    gate, out):
    x3, out3 = x[0], out[0]
    xt_dram = [nc.dram_tensor(f"xt{n}", [HALVES, P, GROUPS, N, GRP], BF16).ap() for n in range(2)]
    x1_dram = nc.dram_tensor("x1", [N, N, C], F32).ap()

    with ExitStack() as ctx:
        def sb(name, shape, dt=F32):
            return ctx.enter_context(nc.sbuf_tensor(name, shape, dt))

        def sem(name):
            return ctx.enter_context(nc.semaphore(name))

        operand = {"lhs": sb("lhs", [P, HALVES, C, P]), "rhs": sb("rhs", [P, HALVES, C, P])}
        quad = sb("quad", [P, P, C])
        chunk = sb("chunk", [P, 2, P * GRP], BF16)

        def row_buffer(seg, j):
            n = j % seg["buffers"]
            if n < 2:
                return chunk[:, n]
            return xin[:, 2 * n - 4:2 * n - 2].rearrange("p b t c -> p (b t c)").bitcast(BF16)

        sig = sb("sig", [P, 2, COLS, C])
        masks = sb("masks", [P, 2, HALVES, N])
        mask_kj, mask_ki = masks[:, 0], masks[:, 1]
        xin = sb("xin", [P, 4, COLS, C])
        xc = sb("xc", [P, 2, COLS, C])
        split = sb("split", [P, 2, COLS, 2, C], BF16)
        gt = split[:, :, :, :, :].bitcast(F32).rearrange("p b t a c -> p b t (a c)")
        xt = sb("xt", [P, 2, GROUPS, GRP, GRP], BF16)
        gchunk = xt[:, 0].rearrange("p g j r -> p (g j r)")
        gspread = [xt[:, 1].rearrange("p g j r -> p (g j r)"),
                   masks[:, :, :, :].rearrange("p a h n -> p (a h n)").bitcast(BF16)]
        opair = sb("opair", [P, COLS // 2, P])
        stats = sb("stats", [P, 2, COLS, 3])
        rstd = sb("rstd", [P, 2, COLS])
        var = sb("var", [P, 2, COLS])
        ident = sb("ident", [P, P])
        ident_b = sb("ident_b", [P, P], BF16)
        ones_b = sb("ones_b", [P, P], BF16)
        w_lhs = [sb(f"w_lhs{n}", [P, 2, 2 * C], BF16) for n in range(2)]
        w_rhs = [sb(f"w_rhs{n}", [P, 2, 2 * C], BF16) for n in range(2)]
        w_gate = sb("w_gate", [P, 2, C], BF16)
        w_out = [sb(f"w_out{n}", [P, P]) for n in range(2)]
        bz_rows = sb("bz_rows", [P, C], BF16)
        ln2 = sb("ln2", [P, 2])
        c_eps = sb("c_eps", [P, COLS])
        minus_half = sb("minus_half", [P, COLS])

        banks = [ctx.enter_context(nc.psum_tensor(f"bank{n}", [P, 2, 512], F32)) for n in range(2)]
        ps_t = ctx.enter_context(nc.psum_tensor("ps_t", [P, COLS // 2, P], F32))
        ps_w = ctx.enter_context(nc.psum_tensor("ps_w", [P, COLS, C], F32))
        ps_x = ctx.enter_context(nc.psum_tensor("ps_x", [P, 2, COLS, P], BF16))
        ps_g = [ps_x[:, n].bitcast(F32).rearrange("p t c -> p (t c)").rearrange(
            "p (t c) -> p t c", c=C) for n in range(2)]

        loaded = sem("loaded")
        zeroed = sem("zeroed")
        idents, basics = sem("idents"), sem("basics")
        prep_v, prep_pe = sem("prep_v"), sem("prep_pe")
        ready = sem("ready")
        x_landed = [sem(f"x_landed{n}") for n in range(4)]
        x_stored = [sem(f"x_stored{n}") for n in range(4)]
        chunk_landed = [sem(f"chunk_landed{n}") for n in range(4)]
        cols_landed = [sem(f"cols_landed{n}") for n in range(2)]
        gchunk_landed = sem("gchunk_landed")
        cols_spread = [sem(f"cols_spread{s}") for s in range(2)]
        gate_spread = sem("gate_spread")
        xt_stored = [sem(f"xt_stored{n}") for n in range(2)]
        stats_done, std_done = sem("stats_done"), sem("std_done")
        centred = [sem(f"centred{n}") for n in range(2)]
        var_done, rstd_done, rooted = sem("var_done"), sem("rstd_done"), sem("rooted")
        normed, high_done, low_done = sem("normed"), sem("high_done"), sem("low_done")
        x_turned, xt_done = sem("x_turned"), sem("xt_done")
        projected, gated, masked, made = sem("projected"), sem("gated"), sem("masked"), sem("made")
        contracted, quad_done = sem("contracted"), sem("quad_done")
        paired, turned, turned_out = sem("paired"), sem("turned"), sem("turned_out")
        mixed, added = sem("mixed"), sem("added")
        gate_mm, gate_sig, scaled, summed = (sem("gate_mm"), sem("gate_sig"), sem("scaled"),
                                             sem("summed"))

        scratch = quad[:, :, :].rearrange("p j c -> p (j c)")
        at = [0]

        landing = [chunk[:, 0], scratch[:, 4 * 1024:5 * 1024].bitcast(BF16)]

        def temp(rows, width):
            at[0] += width
            return scratch[0:rows, at[0] - width:at[0]]

        sets = [
            (w_lhs[0], W_ag, W_ap, b_ag, b_ap, 0), (w_rhs[0], W_bg, W_bp, b_bg, b_bp, 0),
            (w_lhs[1], right1, right2, None, None, 1), (w_rhs[1], left1, left2, None, None, 1),
            (w_gate, gate, None, None, None, 1),
        ]
        raw = [temp(C, C if s[2] is None else 2 * C) for s in sets]
        scaled_w = [temp(C, C if s[2] is None else 2 * C) for s in sets]
        bias_row = [temp(1, 2 * C) if s[3] is not None else None for s in sets]
        norm_w = [temp(C, 1) for _ in range(2)]
        norm_b = [temp(C, 1) for _ in range(2)]
        fold = temp(C, P)
        put_bias = [temp(C, P) for _ in range(2)]
        bz = temp(P, C)
        bz_rest = [temp(P, C) for _ in range(2)]
        bz_part = [temp(P, C // 2).bitcast(BF16) for _ in range(3)]
        prep_ps = [banks[0][:, 0, 0:2 * C], banks[0][:, 1, 0:2 * C], banks[1][:, 0, 0:2 * C],
                   banks[1][:, 1, 0:2 * C], ps_w[:, 0:2, :].rearrange("p a c -> p (a c)")]

        def column(v):
            return v.rearrange("(c a) -> c a", a=1)

        def row(v):
            return v.rearrange("(a c) -> a c", a=1)

        loads = []
        for n, (dst, wg, wv, bg, bv, layer) in enumerate(sets):
            loads.append((raw[n][:, 0:C], wg))
            if wv is not None:
                loads.append((raw[n][:, C:2 * C], wv))
            if bg is not None:
                loads += [(bias_row[n][:, 0:C], row(bg)), (bias_row[n][:, C:2 * C], row(bv))]
        for n, (w, b) in enumerate([(ln_w, ln_b), (ln1_w, ln1_b)]):
            loads += [(norm_w[n], column(w)), (norm_b[n], column(b))]
        for n, v in enumerate((ln2_w, ln2_b)):
            loads += [(ln2[h * C:(h + 1) * C, n:n + 1], column(v)) for h in range(2)]
        loads.append((bz, row(b_z).broadcast_to([P, C])))
        loads.append((mask_kj[:, :, :], mask[0].rearrange("(h p) j -> p h j", p=P)))
        loads_diag = [(w_out[n][h * C:(h + 1) * C, h * C:(h + 1) * C], w)
                      for n, w in enumerate((W_z, out_w)) for h in range(2)]
        LOADED = 16 * (len(loads) + len(loads_diag))
        PER_STEP = -(-len(loads) // (2 * UNROLL))

        def by_group(columns):
            return columns.rearrange("p (g j r) -> p j g r", g=GROUPS, r=GRP)

        def by_vector(columns):
            return columns.rearrange("p (j g r) -> p j g r", g=GROUPS, r=GRP)

        block = ctx.enter_context(nc.Block())

        @block.sync
        def _(sp):
            for s in x_stored:
                sp.sem_inc(s, 16)

            def load_weights(first, count):
                for n in range(first, min(first + count, len(loads))):
                    sp.dma_start(*loads[n]).then_inc(loaded, 16)

            def load_x(seg, r, j):
                kind, rh, ch = seg["norm"]
                if kind != "p":
                    sp.wait_ge(centred[j % 2], after(same_parity(seg, r, j) - 2))
                if kind != "z":
                    sp.wait_ge(x_stored[j], 16 * (r + (seg["m0"] - X_BASE) // 4 + 1))
                src = (x1_dram if kind == "p" else x3)
                cols = bass.ds(ch * P + COLS * number(r, j), COLS)
                sp.dma_start(xin[:, j], src[rh * P:(rh + 1) * P, cols, :]
                             ).then_inc(x_landed[j], 16)

            def load_chunk(seg, r, j):
                layer, _, kind, half = seg["gen"]
                group, other = 2 * r + j % 2, j // 2
                buf = row_buffer(seg, j) if kind == "row" else landing[j % landings(seg)]
                if kind == "col" and not (isinstance(r, int) and (r, j) == (0, 0)):
                    for s in range(2):
                        sp.wait_ge(cols_spread[s],
                                   after(seg["cols0"] + number(r, j) - landings(seg)))
                else:
                    first = isinstance(r, int) and r == 0
                    if seg["buffers"] == 4 and first and j >= 2:
                        for n in range(2):
                            sp.wait_ge(centred[n], after(seg["m0"] // 2 - 1))
                        for n in range(4):
                            sp.wait_ge(x_stored[n], 16 + 16 * (seg["m0"] - X_BASE) // 4)
                    else:
                        back = 2 if first else seg["buffers"]
                        sp.wait_ge(projected, after(2 * (seg["k0"] + number(r, j) - back) + 1))
                    if isinstance(r, int) and (r, j) == (0, 0):
                        for s in range(2):
                            sp.wait_ge(cols_spread[s], after(seg["cols0"] - 1))
                if kind == "row":
                    src = xt_dram[layer][half, :, bass.ds(group, 1), other * P:(other + 1) * P, :]
                    dst = buf.rearrange("p (g j r) -> p g j r", g=1, r=GRP)
                else:
                    src = xt_dram[layer][other, :, :, bass.ds(half * P + GRP * group, GRP), :]
                    dst = buf.rearrange("p (g j r) -> p g j r", g=GROUPS, r=GRP)
                sp.dma_start(dst, src).then_inc(
                    chunk_landed[j % seg["buffers"]] if kind == "row"
                    else cols_landed[j % landings(seg)], 16)

            def load_gate(seg, r, j):
                _, rh, ch = seg["norm"]
                sp.wait_ge(gate_spread, after((seg["m0"] - P_BASE) // 2 + 2 * r + j // 2 - 1))
                sp.dma_start(gchunk.rearrange("p (g j r) -> p g j r", g=GROUPS, r=GRP),
                             xt_dram[1][rh, :, :, bass.ds(ch * P + COLS * number(r, j), GRP), :]
                             ).then_inc(gchunk_landed, 16)

            def store_x(seg, r, j):
                _, rh, ch = seg["norm"]
                sp.wait_ge(added, after(seg["m0"] + number(r, j) - X_BASE))
                cols = bass.ds(ch * P + COLS * number(r, j), COLS)
                sp.dma_start(x1_dram[rh * P:(rh + 1) * P, cols, :],
                             xin[:, j]).then_inc(x_stored[j], 16)

            def store_xt(seg, r, j):
                kind, rh, ch = seg["norm"]
                sp.wait_ge(xt_done, after(seg["m0"] + number(r, j)))
                cols = bass.ds(ch * P + COLS * UNROLL * r + COLS * (j - 1), GRP)
                sp.dma_start(xt_dram[kind == "x"][rh, :, :, cols, :],
                             xt[:, j // 2]).then_inc(xt_stored[j // 2], 16)

            def store_out(seg, r, j):
                _, rh, ch = seg["norm"]
                sp.wait_ge(summed, after(seg["m0"] + number(r, j) - P_BASE))
                cols = bass.ds(ch * P + COLS * number(r, j), COLS)
                sp.dma_start(out3[rh * P:(rh + 1) * P, cols, :],
                              xin[:, j]).then_inc(x_stored[j], 16)

            def wait_stored(seg):
                pairs = min(seg["m0"], P_BASE) // 4
                if pairs:
                    for n in range(2):
                        sp.wait_ge(xt_stored[n], 16 * pairs)
                if seg["m0"] > X_BASE:
                    for n in range(4):
                        sp.wait_ge(x_stored[n], 16 + 16 * (seg["m0"] - X_BASE) // 4)

            def load_step(seg, r, j):
                if seg["gen"]:
                    load_chunk(seg, r, j)
                if seg["norm"] and seg["norm"][0] != "p":
                    load_x(seg, r, j)

            def load_first_steps(seg):
                load_step(seg, 0, 0)
                if loads_two(seg):
                    load_step(seg, 0, 1)

            def loads_two(seg):
                return not (seg["gen"] and seg["gen"][2] == "col" and landings(seg) == 1)

            load_first_steps(SEGMENTS[0])
            carried = None
            for n, seg in enumerate(SEGMENTS):
                kind = seg["norm"] and seg["norm"][0]

                def body(at, tail=False, seg=seg, kind=kind):
                    loaded_before = (loads_two(seg) and at(1) is None) or (
                        seg["buffers"] == 4 and at(3) is None)
                    if at(-1) and not tail and not loaded_before:
                        load_step(seg, *at(-1))
                    if n == 0 and at(0) and isinstance(at(0)[0], int) and not tail:
                        r, j = at(0)
                        load_weights(PER_STEP * (j if r == 0 else UNROLL + j), PER_STEP)
                    if kind == "p" and at(0) and at(0)[1] % 2 == 0:
                        load_gate(seg, *at(0))
                    if kind == "p" and at(4):
                        store_out(seg, *at(4))
                    if kind == "p" and at(2):
                        load_x(seg, *at(2))
                    if kind == "x" and at(2):
                        store_x(seg, *at(2))
                    if kind in ("z", "x") and at(4) and at(4)[1] % 2 == 1:
                        store_xt(seg, *at(4))

                def finish(tail):
                    if n == 0:
                        sp.wait_ge(zeroed, 1)
                        for dst, src in loads_diag:
                            sp.dma_start(dst, src).then_inc(loaded, 16)
                    if n + 1 < len(SEGMENTS):
                        wait_stored(seg)
                        load_first_steps(SEGMENTS[n + 1])
                    for j in range(LAG):
                        tail(j)
                        if j == 1 and n + 1 < len(SEGMENTS) and SEGMENTS[n + 1]["buffers"] == 4:
                            load_step(SEGMENTS[n + 1], 0, 2)
                            load_step(SEGMENTS[n + 1], 0, 3)

                carried = walk(sp, seg, body, finish, carried, ahead=True, hand_on=n == 0)
                if n > 0 and n + 1 < len(SEGMENTS) and SEGMENTS[n + 1]["norm"]:
                    wait_stored(SEGMENTS[n + 1])
            for n in range(4):
                sp.wait_ge(x_stored[n], 16 + 16 * (3 * 4 * STEPS - X_BASE) // 4)

        @block.gpsimd
        def _(pool):
            g = nc.gpsimd
            for s in (*centred, masked, summed, var_done, rooted):
                pool.sem_inc(s, START)
            g.memset(ident[:, :], 0.0).then_inc(idents, 1)
            for n in range(2):
                last = g.memset(w_out[n][:, :], 0.0)
            last.then_inc(zeroed, 1)
            g.memset(minus_half[:, :], -0.5)
            g.memset(c_eps[:, :], C * EPS).then_inc(idents, 1)
            g.memset(ones_b[:, :], 1.0)
            pool.wait_ge(idents, 2)
            g.affine_select(out=ident[:, :], in_=ident[:, :], compare_op=ALU.not_equal, fill=1.0,
                            base=0, pattern=[[-1, P]], channel_multiplier=1).then_inc(idents, 1)

            def mask_gate(seg, r, j, s):
                layer, op, kind, half = seg["gen"]
                group, other = 2 * r + j % 2, j // 2
                table = mask_ki if kind == "row" else mask_kj
                pool.wait_ge(gated, after(2 * (seg["k0"] + number(r, j)) + s))
                m8 = table[:, other, bass.ds(half * P + GRP * group + COLS * s, COLS)].unsqueeze(2)
                g.tensor_tensor(sig[:, s], sig[:, s], m8.broadcast_to([P, COLS, C]),
                                ALU.mult).then_inc(masked, 1)

            def centre(seg, r, j):
                m, h = seg["m0"] + number(r, j), j % 2
                pool.wait_ge(stats_done, after(m))
                if seg["norm"][0] == "p":
                    pool.wait_ge(turned, after(m - X_BASE - 2))
                    src, lo = quad[:, bass.ds(COLS * number(r, j), COLS), :], 0
                else:
                    pool.wait_ge(low_done, after(m - 2))
                    src, lo = xin[:, j], 1
                g.tensor_tensor(xc[:, h, :, lo:], src[:, :, lo:],
                                stats[:, h, :, 1:2].broadcast_to([P, COLS, C - lo]),
                                ALU.subtract).then_inc(centred[h], 1)

            def root(seg, r, j):
                m, h = seg["m0"] + number(r, j), j % 2
                pool.wait_ge(normed, after(m - 2))
                pool.wait_ge(stats_done, after(m))
                g.tensor_tensor(var[:, h], stats[:, h, :, 2], c_eps[:, :], ALU.add
                                ).then_inc(var_done, 1)
                pool.wait_ge(var_done, after(m - SQRT_STEPS))
                g.tensor_tensor(rstd[:, h], var[:, h], minus_half[:, :], ALU.pow
                                ).then_inc(rooted, 1)

            def add_residual(seg, r, j):
                m, h = seg["m0"] + number(r, j), j % 2
                pool.wait_ge(scaled, after(m - P_BASE))
                pool.wait_ge(x_landed[j], landed(seg, r))
                g.tensor_tensor(xin[:, j], xin[:, j], gt[:, h], ALU.add).then_inc(summed, 1)

            carried = None
            for seg in SEGMENTS:
                masks_gates = seg["gen"] and seg["gen"][0] == 0
                if seg is FIRST_GEN:
                    pool.wait_ge(ready, 1)

                def body(at, tail=False, seg=seg, masks_gates=masks_gates):
                    if masks_gates and at(1) and not tail:
                        mask_gate(seg, *at(1), 1)
                    lag = 0 if seg["norm"] and seg["norm"][0] == "p" else 1
                    if seg["norm"] and at(lag):
                        if not sqrt_on_act(seg):
                            root(seg, *at(lag))
                        if not centre_on_vector(seg, at(lag)[1]):
                            centre(seg, *at(lag))
                    if seg["norm"] and seg["norm"][0] == "p" and at(3):
                        add_residual(seg, *at(3))
                    if masks_gates and at(0):
                        mask_gate(seg, *at(0), 0)

                def finish(tail):
                    if masks_gates:
                        mask_gate(seg, ROUNDS - 1, UNROLL - 1, 1)
                    for j in range(LAG):
                        tail(j)

                carried = walk(pool, seg, body, finish, carried)

        @block.scalar
        def _(act):
            a = nc.scalar
            for s in (std_done, high_done, xt_done, gated, quad_done, paired, turned_out, gate_sig):
                act.sem_inc(s, START)
            act.wait_ge(idents, 3)

            def spread_cols(seg, r, j):
                act.wait_ge(cols_landed[0], columns_landed(seg, r, j))
                act.wait_ge(projected, after(2 * (seg["k0"] + number(r, j) - 1) + 1))
                a.activation(by_vector(chunk[:, 1])[:, COLS:], by_group(landing[0])[:, COLS:],
                             ACT.Copy).then_inc(cols_spread[1], 1)

            def gates(seg, r, j, s):
                n = 2 * (seg["k0"] + number(r, j)) + s
                act.wait_ge(projected, after(n))
                act.wait_ge(made, after(n - 2))
                v = banks[s][:, :, :].rearrange("p b (t c) -> p (b t) c", c=2 * C)
                a.activation(sig[:, s], v[:, :, 0:C], ACT.Sigmoid).then_inc(gated, 1)

            def std(seg, r, j):
                m, h = seg["m0"] + number(r, j), j % 2
                act.wait_ge(stats_done, after(m))
                act.wait_ge(normed, after(m - 2))
                a.activation(var[:, h], stats[:, h, :, 2], ACT.Sqrt, bias=c_eps[:, 0:1]
                             ).then_inc(std_done, 1)

            def high(seg, r, j):
                m, h = seg["m0"] + number(r, j), j % 2
                act.wait_ge(normed, after(m))
                act.wait_ge(x_turned, after(m - 2))
                a.activation(split[:, h, :, 0, 1:], xc[:, h, :, 1:], ACT.Copy
                             ).then_inc(high_done, 1)

            def pair_up(seg, r, j):
                o = seg["m0"] - X_BASE + number(r, j)
                act.wait_ge(mixed, after(o - 1))
                a.activation(opair[:, :, :].rearrange("p a (b c) -> p (a b) c", c=C),
                             quad[:, bass.ds(COLS * number(r, j), COLS), :], ACT.Copy).then_inc(paired, 1)

            def turn_out(seg, r, j):
                o = seg["m0"] - X_BASE + number(r, j)
                act.wait_ge(turned, after(o))
                if seg["norm"][0] == "x":
                    a.activation(opair[:, :, :], ps_t[:, :, :], ACT.Copy).then_inc(turned_out, 1)
                else:
                    act.wait_ge(mixed, after(o - 1))
                    a.activation(opair[:, :, :], ps_t[:, :, :], ACT.Identity, scale=ln2[:, 0:1],
                                 bias=ln2[:, 1:2]).then_inc(turned_out, 1)

            def xt_out(seg, r, j):
                m, h = seg["m0"] + number(r, j), j % 2
                act.wait_ge(x_turned, after(m))
                if not (isinstance(m, int) and m < 4):
                    act.wait_ge(xt_stored[j // 2], 16 * (seg["m0"] // 4 + r))
                a.activation(xt[:, j // 2, :, COLS * h:COLS * (h + 1), :].rearrange("p g j r -> p j g r"),
                              ps_x[:, h].rearrange("p j (g r) -> p j g r", r=GRP), ACT.Copy).then_inc(xt_done, 1)

            def gate_out(seg, r, j):
                n, h = seg["m0"] - P_BASE + number(r, j), j % 2
                act.wait_ge(gate_mm, after(n))
                act.wait_ge(summed, after(n - 2))
                a.activation(gt[:, h], ps_g[h], ACT.Sigmoid).then_inc(gate_sig, 1)

            def fill_quadrant(seg, n):
                if n == 0 and seg["norm"] and seg["norm"][0] == "p":
                    for h in range(2):
                        act.wait_ge(centred[h], after((seg["m0"] + STEPS) // 2 - 1))
                act.wait_ge(contracted, after(seg["e0"] + n))
                a.activation(quad[:, :, n * CG:(n + 1) * CG],
                             banks[n % 2][:, :, :].rearrange("p b (c j) -> p j (b c)", j=P),
                             ACT.Copy).then_inc(quad_done, 1)

            carried = None
            for seg in SEGMENTS:
                kind = seg["norm"] and seg["norm"][0]
                if seg is FIRST_GEN:
                    act.wait_ge(ready, 1)
                if kind == "x":
                    act.wait_ge(quad_done, after(seg["e0"] - 1))
                if kind == "p":
                    act.wait_ge(x_turned, after(P_BASE - 1))

                def body(at, tail=False, seg=seg, kind=kind):
                    if kind == "x" and at(0):
                        pair_up(seg, *at(0))
                    if seg["gen"] and at(1) and not tail:
                        gates(seg, *at(1), 1)
                    if seg["gen"] and seg["gen"][2] == "col" and landings(seg) == 1 and at(0):
                        spread_cols(seg, *at(0))
                    if kind == "p" and at(3):
                        gate_out(seg, *at(3))
                    if sqrt_on_act(seg) and at(1):
                        std(seg, *at(1))
                    if kind == "x" and at(0):
                        turn_out(seg, *at(0))
                    if kind in ("z", "x") and at(2):
                        high(seg, *at(2))
                    if kind == "p" and at(2):
                        turn_out(seg, *at(2))
                    if seg["gen"] and at(0):
                        gates(seg, *at(0), 0)
                    if kind in ("z", "x") and at(3):
                        xt_out(seg, *at(3))

                def finish(tail):
                    if seg["gen"]:
                        gates(seg, ROUNDS - 1, UNROLL - 1, 1)
                    for n in range(GROUPS_C):
                        tail(n)
                        if seg["contract"]:
                            fill_quadrant(seg, n)

                carried = walk(act, seg, body, finish, carried)

        @block.vector
        def _(dve):
            v = nc.vector
            for s in (stats_done, rstd_done, normed, low_done, made, added, scaled,
                      *cols_spread, gate_spread):
                dve.sem_inc(s, START)
            chain = [0]
            def link(ins):
                chain[0] += 1
                ins.then_inc(prep_v, 1)
                dve.wait_ge(prep_v, chain[0])

            for h in range(2):
                v.memset(split[:, h, :, 0, 0:1], 1.0)
                v.memset(split[:, h, :, 1, 0:1], 0.0)
            dve.wait_ge(idents, 3)
            v.tensor_copy(ident_b[:, :], ident[:, :]).then_inc(basics, 1)

            def prepare():
                v.memset(fold, 0.0)
                for n in range(2):
                    v.memset(put_bias[n], 0.0)
                link(v.memset(bz_rows[:, :], 0.0))
                for h in range(2):
                    last = v.tensor_scalar(fold[:, h * C + 1:(h + 1) * C], ident[0:C, 1:C], ROOT_C, None,
                                           ALU.mult)
                link(last)
                for h in range(2):
                    v.memset(fold[0:1, h * C + 1:(h + 1) * C], -ROOT_C)
                dve.wait_ge(loaded, LOADED)
                for n in range(2):
                    v.tensor_copy(put_bias[n][:, 0:1], norm_b[n])
                for n, s in enumerate(sets):
                    last = v.tensor_scalar(scaled_w[n], raw[n], norm_w[s[5]], None, ALU.mult)
                link(last)
                link(v.tensor_copy(bz_part[0], bz))
                link(v.tensor_tensor(bz_rest[0], bz, bz_part[0], ALU.subtract))
                link(v.tensor_copy(bz_part[1], bz_rest[0]))
                link(v.tensor_tensor(bz_rest[1], bz_rest[0], bz_part[1], ALU.subtract))
                link(v.tensor_copy(bz_part[2], bz_rest[1]))
                for n in range(3):
                    v.tensor_copy(bz_rows[32 * n:32 * n + 1, :], bz_part[n][32 * n:32 * n + 1, :])

            def keep_prepared():
                dve.wait_ge(prep_pe, 1)
                for n, s in enumerate(sets):
                    w = C if s[2] is None else 2 * C
                    last = v.tensor_copy(s[0][:, 0, :], prep_ps[n][:, 0:w])
                v.tensor_copy(mask_ki[:, 0, :], ps_t[:, 0:2, :].rearrange("p a b -> p (a b)"))
                v.tensor_copy(mask_ki[:, 1, :], ps_t[:, 2:4, :].rearrange("p a b -> p (a b)"))
                link(v.tensor_scalar(ln2[:, 0:1], ln2[:, 0:1], ROOT_C, None, ALU.mult))
                for n, s in enumerate(sets):
                    w = C if s[2] is None else 2 * C
                    last = v.tensor_tensor(s[0][:, 1, :], prep_ps[n][:, 0:w], s[0][:, 0, :],
                                           ALU.subtract)
                last.then_inc(ready, 1)

            def spread_cols(seg, r, j):
                dve.wait_ge(cols_landed[j % landings(seg)], columns_landed(seg, r, j))
                for s in range(landings(seg)):
                    dve.wait_ge(projected, after(2 * (seg["k0"] + number(r, j) - 1) + s))
                    eight = slice(COLS * s, COLS * (s + 1))
                    v.tensor_copy(by_vector(chunk[:, 1])[:, eight],
                                  by_group(landing[j % landings(seg)])[:, eight]
                                  ).then_inc(cols_spread[s], 1)

            def spread_gate(seg, r, j):
                w = (seg["m0"] - P_BASE) // 2 + 2 * r + j // 2
                dve.wait_ge(gchunk_landed, 16 * (w + 1))
                dve.wait_ge(gate_mm, after(2 * w - 3))
                v.tensor_copy(by_vector(gspread[j // 2]), by_group(gchunk)).then_inc(gate_spread, 1)

            def make(seg, r, j, s):
                layer, op, kind, half = seg["gen"]
                group, other = 2 * r + j % 2, j // 2
                if isinstance(r, int) and (r, j, s) == (0, 0, 0) and seg["e0"]:
                    dve.wait_ge(contracted, after(seg["e0"] - 1))
                dve.wait_ge(masked if layer == 0 else gated, after(2 * (seg["k0"] + number(r, j)) + s))
                dst = operand[op][:, other, :, bass.ds(GRP * group + COLS * s, COLS)]
                ps = banks[s][:, :, :].rearrange("p b (t c) -> p c (b t)", c=2 * C)
                v.tensor_tensor(dst, ps[:, C:2 * C, :], sig[:, s].rearrange("p t c -> p c t"),
                                ALU.mult).then_inc(made, 1)

            def statistics(seg, r, j):
                kind = seg["norm"][0]
                m, h = seg["m0"] + number(r, j), j % 2
                dve.wait_ge(centred[h], after(same_parity(seg, r, j) - 1))
                if kind == "z":
                    dve.wait_ge(x_landed[j], landed(seg, r))
                if kind == "x":
                    dve.wait_ge(added, after(m - X_BASE))
                for c in range(0, COLS, 2):
                    if kind == "p":
                        src = quad[:, bass.ds(COLS * number(r, j) + c, 2), :]
                    else:
                        src = xin[:, j, c:c + 2, :]
                    last = v.bn_stats(stats[:, h, c:c + 2, :].rearrange("p a s -> p (a s)"),
                                      src.rearrange("p a c -> p c a"))
                last.then_inc(stats_done, 1)

            def add(seg, r, j):
                dve.wait_ge(mixed, after(seg["m0"] - X_BASE + number(r, j)))
                dve.wait_ge(x_landed[j], landed(seg, r))
                v.tensor_tensor(xin[:, j], xin[:, j], ps_w[:, :, :], ALU.add).then_inc(added, 1)

            def centre(seg, r, j):
                m, h = seg["m0"] + number(r, j), j % 2
                if seg["norm"][0] == "p":
                    dve.wait_ge(turned, after(m - X_BASE - 2))
                    src, lo = quad[:, bass.ds(COLS * number(r, j), COLS), :], 0
                else:
                    dve.wait_ge(low_done, after(m - 2))
                    src, lo = xin[:, j], 1
                dve.wait_ge(stats_done, after(m))
                v.tensor_tensor(xc[:, h, :, lo:], src[:, :, lo:],
                                stats[:, h, :, 1:2].broadcast_to([P, COLS, C - lo]),
                                ALU.subtract).then_inc(centred[h], 1)

            def normalise(seg, r, j):
                m, h = seg["m0"] + number(r, j), j % 2
                dve.wait_ge(centred[h], after(same_parity(seg, r, j)))
                if not sqrt_on_act(seg):
                    dve.wait_ge(rooted, after(m - SQRT_STEPS))
                if sqrt_on_act(seg):
                    dve.wait_ge(std_done, after(m))
                    v.reciprocal(rstd[:, h], var[:, h]).then_inc(rstd_done, 1)
                    dve.wait_ge(rstd_done, after(m))
                lo = 0 if seg["norm"][0] == "p" else 1
                v.tensor_tensor(xc[:, h, :, lo:], xc[:, h, :, lo:],
                                rstd[:, h].unsqueeze(2).broadcast_to([P, COLS, C - lo]),
                                ALU.mult).then_inc(normed, 1)

            def low(seg, r, j):
                m, h = seg["m0"] + number(r, j), j % 2
                dve.wait_ge(high_done, after(m))
                v.tensor_tensor(split[:, h, :, 1, 1:], xc[:, h, :, 1:], split[:, h, :, 0, 1:],
                                ALU.subtract).then_inc(low_done, 1)

            def scale(seg, r, j):
                n, h = seg["m0"] - P_BASE + number(r, j), j % 2
                dve.wait_ge(gate_sig, after(n))
                dve.wait_ge(mixed, after(seg["m0"] - X_BASE + number(r, j)))
                v.tensor_tensor(gt[:, h], ps_w[:, :, :], gt[:, h], ALU.mult).then_inc(scaled, 1)

            carried = None
            for seg in SEGMENTS:
                kind = seg["norm"] and seg["norm"][0]
                if seg is FIRST_GEN:
                    keep_prepared()
                if seg["e0"] and kind == "p":
                    dve.wait_ge(quad_done, after(seg["e0"] - 1))

                def body(at, tail=False, seg=seg, kind=kind):
                    if seg["gen"] and seg["gen"][2] == "col" and at(0):
                        spread_cols(seg, *at(0))
                    if kind == "x" and at(1):
                        statistics(seg, *at(1))
                    if kind in ("z", "p") and at(0):
                        statistics(seg, *at(0))
                    if seg["gen"] and at(1) and not tail:
                        make(seg, *at(1), 1)
                    if kind and at(1) and centre_on_vector(seg, at(1)[1]):
                        centre(seg, *at(1))
                    if kind in ("z", "x") and at(2):
                        low(seg, *at(2))
                    if kind == "x" and at(0):
                        add(seg, *at(0))
                    if kind == "p" and at(3):
                        scale(seg, *at(3))
                    if kind and at(1) and not centre_on_pool(seg):
                        normalise(seg, *at(1))
                    if seg["gen"] and at(0):
                        make(seg, *at(0), 0)
                    if kind and at(1) and centre_on_pool(seg):
                        normalise(seg, *at(1))
                    if kind == "p" and at(1) and at(1)[1] % 2 == 0:
                        spread_gate(seg, *at(1))
                    if seg is SEGMENTS[1] and not tail and first_round(at) and at(0)[1] == 1:
                        prepare()

                def finish(tail):
                    if seg["gen"]:
                        make(seg, ROUNDS - 1, UNROLL - 1, 1)
                    for j in range(LAG):
                        tail(j)

                carried = walk(dve, seg, body, finish, carried)

        @block.tensor
        def _(pe):
            mm = nc.tensor.matmul
            for s in (x_turned, projected, contracted, turned, mixed, gate_mm):
                pe.sem_inc(s, START)
            pe.wait_ge(basics, 1)

            def prepare(part):
                PREPARED = 4
                pe.wait_ge(prep_v, PREPARED)
                pe.wait_ge(loaded, LOADED)
                for n, s in enumerate(sets):
                    if n // 3 != part:
                        continue
                    w = C if s[2] is None else 2 * C
                    dst = prep_ps[n][:, 0:w]
                    mm(dst, fold, scaled_w[n], start=True, stop=False)
                    mm(dst, put_bias[s[5]], raw[n], start=False, stop=s[3] is None)
                    if s[3] is not None:
                        mm(dst, ident[0:1, :], bias_row[n], start=False, stop=True)
                if part == 0:
                    return
                for kh in range(HALVES):
                    for ih in range(HALVES):
                        last = nc.tensor.transpose(ps_t[:, 2 * kh + ih, :],
                                                   mask_kj[:, ih, kh * P:(kh + 1) * P], ident[:, :])
                last.then_inc(prep_pe, 1)

            def project(seg, r, j, s):
                layer, op, kind, half = seg["gen"]
                k = seg["k0"] + number(r, j)
                if s == 0 and kind == "row":
                    pe.wait_ge(chunk_landed[j % seg["buffers"]], chunks_landed(seg, r, j))
                if kind == "col":
                    pe.wait_ge(cols_spread[s], after(seg["cols0"] + number(r, j)))
                pe.wait_ge(made, after(2 * k + s - 2))
                if isinstance(r, int) and (r, j) == (0, 0) and seg["e0"]:
                    pe.wait_ge(quad_done, after(seg["e0"] - 2 + s))
                w = (w_lhs if op == "lhs" else w_rhs)[layer]
                ps = banks[s][:, :, :].rearrange("p b (t c) -> p (b t) c", c=2 * C)
                for n in range(COLS):
                    vec = COLS * s + n
                    if kind == "row":
                        x_vec = row_buffer(seg, j).rearrange("p (j r) -> p j r", r=GRP)[:, :, vec]
                    else:
                        x_vec = chunk[:, 1].rearrange("p (j r) -> p j r", r=P)[:, vec, :]
                    mm(ps[:, n, :], x_vec, w[:, 0, :], start=True, stop=False)
                    last = mm(ps[:, n, :], x_vec, w[:, 1, :], start=False, stop=True)
                last.then_inc(projected, 1)

            def contract(seg, group):
                if group == 0:
                    pe.wait_ge(made, after(2 * (seg["k0"] + CHUNKS) - 1))
                pe.wait_ge(quad_done, after(seg["e0"] + group - 2))
                for n in range(CG):
                    dst = banks[group % 2][:, :, :].rearrange("p b (c j) -> p (b c) j", j=P)[:, n]
                    for kh in range(HALVES):
                        last = mm(dst, operand["lhs"][:, kh, group * CG + n, :],
                                  operand["rhs"][:, kh, group * CG + n, :],
                                  start=kh == 0, stop=kh == HALVES - 1)
                last.then_inc(contracted, 1)

            def turn(seg, r, j):
                o = seg["m0"] - X_BASE + number(r, j)
                pe.wait_ge(turned_out, after(o - 1))
                if seg["norm"][0] == "x":
                    pe.wait_ge(paired, after(o))
                    src = opair[:, :, :]
                else:
                    pe.wait_ge(normed, after(seg["m0"] + number(r, j)))
                    src = xc[:, j % 2].rearrange("p (a b) c -> p a (b c)", b=2)
                for n in range(COLS // 2):
                    last = nc.tensor.transpose(ps_t[:, n, :], src[:, n, :], ident[:, :])
                last.then_inc(turned, 1)

            def mix(seg, r, j):
                o = seg["m0"] - X_BASE + number(r, j)
                pe.wait_ge(turned_out, after(o))
                if seg["norm"][0] == "x":
                    layer = 0
                    pe.wait_ge(added, after(o - 1))
                    mm(ps_w[:, :, :], ones_b[:, :],
                       bz_rows[:, :].unsqueeze(1).broadcast_to([P, COLS, C]), start=True, stop=True)
                else:
                    layer = 1
                    pe.wait_ge(scaled, after(o - 4 * STEPS - 1))
                for n in range(COLS // 2):
                    last = mm(ps_w[:, 2 * n:2 * n + 2, :], opair[:, n, :], w_out[layer][:, :],
                              start=layer == 1, stop=True,
                              skip_group_check=layer == 0)
                last.then_inc(mixed, 1)

            def turn_x(seg, r, j):
                m, h = seg["m0"] + number(r, j), j % 2
                pe.wait_ge(low_done, after(m))
                pe.wait_ge(xt_done, after(m - 2))
                for n in range(COLS):
                    last = nc.tensor.transpose(ps_x[:, h, n, :],
                                               split[:, h, n].rearrange("p a c -> p (a c)"),
                                               ident_b[:, :])
                last.then_inc(x_turned, 1)

            def gate_product(seg, r, j):
                n, h = seg["m0"] - P_BASE + number(r, j), j % 2
                if h == 0:
                    pe.wait_ge(gate_spread, after((seg["m0"] - P_BASE) // 2 + 2 * r + j // 2))
                pe.wait_ge(gate_sig, after(n - 2))
                for c in range(COLS):
                    x_vec = gspread[j // 2].rearrange("p (j r) -> p j r", r=P)[:, COLS * h + c, :]
                    mm(ps_g[h][:, c, :], x_vec, w_gate[:, 0, :], start=True, stop=False)
                    last = mm(ps_g[h][:, c, :], x_vec, w_gate[:, 1, :], start=False, stop=True)
                last.then_inc(gate_mm, 1)

            carried = None
            for seg in SEGMENTS:
                kind = seg["norm"] and seg["norm"][0]
                if seg is FIRST_GEN:
                    pe.wait_ge(ready, 1)
                if kind == "p":
                    pe.wait_ge(xt_done, after(P_BASE - 1))

                def body(at, tail=False, seg=seg, kind=kind):
                    first = not tail and at(1) is None
                    if seg["gen"] and at(0) and first:
                        project(seg, *at(0), 0)
                    if kind == "x" and at(0):
                        turn(seg, *at(0))
                    if kind == "p" and at(2):
                        turn(seg, *at(2))
                    if seg["gen"] and at(0) and not first:
                        project(seg, *at(0), 0)
                    if kind == "x" and at(0):
                        mix(seg, *at(0))
                    if kind == "p" and at(2):
                        gate_product(seg, *at(2))
                    if seg["gen"] and at(0):
                        project(seg, *at(0), 1)
                    if kind == "p" and at(2):
                        mix(seg, *at(2))
                    if kind in ("z", "x") and at(2):
                        turn_x(seg, *at(2))
                    if seg is SEGMENTS[1] and not tail and first_round(at) and at(0)[1] >= 2:
                        prepare(at(0)[1] - 2)

                def finish(tail):
                    for n in range(GROUPS_C):
                        if seg["contract"]:
                            contract(seg, n)
                        tail(n)

                carried = walk(pe, seg, body, finish, carried)


SQRT_STEPS = sum(STEPS for s in SEGMENTS if s["norm"] and s["norm"][0] == "z" and not s["gen"])


def sqrt_on_act(seg):
    return bool(seg["norm"]) and seg["norm"][0] == "z" and not seg["gen"]


def centre_on_pool(seg):
    return sqrt_on_act(seg) or (seg["norm"][0] == "x" and seg["gen"][0] == 1)


def centre_on_vector(seg, j):
    if centre_on_pool(seg):
        return False
    return not (seg["gen"] and seg["norm"][0] == "p") or j % 2 == 1


def same_parity(seg, r, j):
    return seg["m0"] // 2 + 2 * r + j // 2


def landings(seg):
    return 2 if seg["m0"] < X_BASE else 1


def columns_landed(seg, r, j):
    if landings(seg) == 2:
        return 16 * (2 * r + j // 2 + 1)
    return 16 * (seg["cols0"] // 2 + number(r, j) + 1)


def chunks_landed(seg, r, j):
    if seg["buffers"] == 4:
        return 16 * ((seg["rows0"] if j < 2 else 0) + r + 1)
    return 16 * (seg["rows0"] + 2 * r + j // 2 + 1)


def landed(seg, r):
    return 16 * (seg["m0"] // 4 + r + 1)


_INS = ['x', 'L0_conv_mask', 'L0_conv_ln_w', 'L0_conv_ln_b', 'L0_conv_W_ap', 'L0_conv_b_ap',
        'L0_conv_W_ag', 'L0_conv_b_ag', 'L0_conv_W_bp', 'L0_conv_b_bp', 'L0_conv_W_bg',
        'L0_conv_b_bg', 'L0_conv_W_z', 'L0_conv_b_z', 'L1_conv_ln1_w', 'L1_conv_ln1_b',
        'L1_conv_left1', 'L1_conv_left2', 'L1_conv_right1', 'L1_conv_right2', 'L1_conv_ln2_w',
        'L1_conv_ln2_b', 'L1_conv_out_w', 'L1_conv_gate']
_OUTS = [((1, 256, 256, 64), 'float32')]


def kernel(**inputs):
    import numpy as _np
    import concourse.bacc as _bacc
    from concourse import mybir as _mybir
    from concourse.bass_utils import run_bass_kernel_spmd as _run

    nc = _bacc.Bacc("TRN2", target_bir_lowering=False, num_devices=1)
    arrays, args = {}, []
    for name in _INS:
        a = _np.ascontiguousarray(inputs[name])
        arrays[f"in_{name}_dram"] = a
        args.append(nc.dram_tensor(f"in_{name}_dram", a.shape, _mybir.dt.from_np(a.dtype), kind="ExternalInput").ap())
    for i, (shape, dtype) in enumerate(_OUTS):
        dt = _mybir.dt.from_np(_np.dtype(dtype))
        args.append(nc.dram_tensor(f"out_{i}_dram", shape, dt, kind="ExternalOutput").ap())
    triangle_layers(nc, *args)
    r = _run(nc, [arrays], core_ids=[0])
    got = tuple(r.results[0][f"out_{i}_dram"] for i in range(len(_OUTS)))
    return got[0]
```
